# Optimizing a Trainium2 kernel written in Bass

```python
import numpy as np
import jax
import jax.numpy as jnp

def _softmax(x, axis=-1):
    return jax.nn.softmax(x, axis=axis)

def _gelu(x):
    return jax.nn.gelu(x, approximate=True)

def _silu(x):
    return jax.nn.silu(x)

def _sigmoid(x):
    return jax.nn.sigmoid(x)

def _layernorm(x, axis=-1, eps=1e-05):
    m = jnp.mean(x, axis=axis, keepdims=True)
    v = jnp.var(x, axis=axis, keepdims=True)
    return (x - m) / jnp.sqrt(v + eps)

def _scatter_add(tgt, idx, src, axis=0):
    return tgt.at[idx].add(src)

def _segment_sum(src, seg, n):
    return jax.ops.segment_sum(src, seg, n)
kernel_name = 'mk_decoder_preln_d1_seqx_r4_13fee8'

def setup_inputs(seed: int=0):
    np.random.seed(seed)
    _w = jnp.asarray

    def _rec_inputs():
        import jax
        import jax.numpy as jnp
        _rk = jax.random.key(seed)
        x = -0.0002928 + 1 * jax.random.normal(jax.random.fold_in(_rk, 1), (16, 128, 256), jnp.float32)
        _lenS = 128 - jax.random.randint(jax.random.fold_in(_rk, 7), (16,), 0, max(1, 128 // 4) + 1, jnp.int32)
        _lenS2 = 128 - jax.random.randint(jax.random.fold_in(_rk, 8), (16,), 0, max(1, 128 // 4) + 1, jnp.int32)
        _ctx_1024P = jax.random.normal(jax.random.fold_in(_rk, 11), (16, 16, 256), jnp.float32)
        _ctx_1024c = jax.random.dirichlet(jax.random.fold_in(_rk, 511), 0.3 * jnp.ones((16,), jnp.float32), (16, 128))
        _ctx_1024t = jnp.einsum('bsk,bkd->bsd', _ctx_1024c, _ctx_1024P)
        _ctx_1024t = _ctx_1024t * jax.lax.rsqrt(jnp.mean(jnp.square(_ctx_1024t)) + 1e-12) * 0.953939
        ctx_1024 = -1.39393e-06 + 0.999914 * (_ctx_1024t + 0.3 * jax.random.normal(jax.random.fold_in(_rk, 611), (16, 128, 256), jnp.float32))
        return (x, ctx_1024)
    x, ctx_1024 = _rec_inputs()

    def _L0_attn_setup():
        import jax, jax.numpy as jnp
        import numpy as np
        H = 8
        HD = 64
        WIN = 64
        key = jax.random.key(seed)
        k1, k2, k3 = jax.random.split(key, 3)
        B, T, D = (1, 1024, 256)
        inner = H * HD
        x = jax.random.normal(k1, (B, T, D), dtype=jnp.float32)
        Wqkv = jax.random.normal(k2, (D, 3 * inner), dtype=jnp.float32) * D ** (-0.5)
        Wout = jax.random.normal(k3, (inner, D), dtype=jnp.float32) * inner ** (-0.5)
        return {'x': x, 'Wqkv': Wqkv, 'Wout': Wout}
    _L0_attn_all = _L0_attn_setup()
    _L0_attn_in = {k: v for k, v in _L0_attn_all.items() if k in ('Wqkv', 'Wout')}
    del _L0_attn_all

    def _L0_xattn_setup():
        import math
        import jax, jax.numpy as jnp
        import numpy as np
        H = 16
        D_MODEL = 256
        D_K = 64
        D_V = 64
        key = jax.random.key(seed)
        ks = jax.random.split(key, 7)
        b, n = (2, 512)
        scale = 1.0 / math.sqrt(D_MODEL)
        return {'q': jax.random.normal(ks[0], (b, n, D_MODEL), jnp.float32), 'k': jax.random.normal(ks[1], (b, n, D_MODEL), jnp.float32), 'v': jax.random.normal(ks[2], (b, n, D_MODEL), jnp.float32), 'w_q': jax.random.normal(ks[3], (H * D_K, D_MODEL), jnp.float32) * scale, 'w_k': jax.random.normal(ks[4], (H * D_K, D_MODEL), jnp.float32) * scale, 'w_v': jax.random.normal(ks[5], (H * D_V, D_MODEL), jnp.float32) * scale, 'w_o': jax.random.normal(ks[6], (D_MODEL, H * D_V), jnp.float32) * scale}
    _L0_xattn_all = _L0_xattn_setup()
    _L0_xattn_in = {k: v for k, v in _L0_xattn_all.items() if k in ('w_q', 'w_k', 'w_v', 'w_o')}
    del _L0_xattn_all

    def _L0_ffn_setup():
        import jax, jax.numpy as jnp
        import numpy as np
        EPS = 1e-06
        LN_EPS = 1e-05

        def _absmean_core(W):
            gamma = jnp.mean(jnp.abs(W)) + EPS
            Ws = W / gamma
            Wq = jnp.sign(Ws) * jnp.minimum(jnp.round(jnp.abs(Ws)), 1.0)
            return (Wq, gamma)

        @jax.custom_vjp
        def absmean(W):
            return _absmean_core(W)[0]

        def _absmean_fwd(W):
            Wq, gamma = _absmean_core(W)
            return (Wq, gamma)

        def _absmean_bwd(gamma, g):
            return (g / gamma,)
        absmean.defvjp(_absmean_fwd, _absmean_bwd)

        def layernorm(x, w, b, eps=LN_EPS):
            mu = jnp.mean(x, axis=-1, keepdims=True)
            var = jnp.mean((x - mu) ** 2, axis=-1, keepdims=True)
            return (x - mu) * jax.lax.rsqrt(var + eps) * w + b
        key = jax.random.key(seed)
        k1, k2, k3 = jax.random.split(key, 3)
        d, h = (256, 1024)
        B, T = (8, 512)
        return {'x': jax.random.normal(k1, (B, T, d), jnp.float32), 'W_fc': jax.random.normal(k2, (h, d), jnp.float32), 'ln_w': jnp.ones((h,), jnp.float32), 'ln_b': jnp.zeros((h,), jnp.float32), 'W_proj': jax.random.normal(k3, (d, h), jnp.float32)}
    _L0_ffn_all = _L0_ffn_setup()
    _L0_ffn_in = {k: v for k, v in _L0_ffn_all.items() if k in ('W_fc', 'ln_w', 'ln_b', 'W_proj')}
    del _L0_ffn_all
    return {'x': x, 'ctx_1024': ctx_1024, 'L0_attn_Wqkv': _L0_attn_in['Wqkv'], 'L0_attn_Wout': _L0_attn_in['Wout'], 'L0_xattn_w_q': _L0_xattn_in['w_q'], 'L0_xattn_w_k': _L0_xattn_in['w_k'], 'L0_xattn_w_v': _L0_xattn_in['w_v'], 'L0_xattn_w_o': _L0_xattn_in['w_o'], 'L0_ffn_W_fc': _L0_ffn_in['W_fc'], 'L0_ffn_ln_w': _L0_ffn_in['ln_w'], 'L0_ffn_ln_b': _L0_ffn_in['ln_b'], 'L0_ffn_W_proj': _L0_ffn_in['W_proj']}

def reference(x, ctx_1024, L0_attn_Wqkv, L0_attn_Wout, L0_xattn_w_q, L0_xattn_w_k, L0_xattn_w_v, L0_xattn_w_o, L0_ffn_W_fc, L0_ffn_ln_w, L0_ffn_ln_b, L0_ffn_W_proj):
    import jax
    import jax.numpy as jnp

    def _L0_attn_ref(x, Wqkv, Wout):
        import jax, jax.numpy as jnp
        import numpy as np
        H = 8
        HD = 64
        WIN = 64
        B, T, D = x.shape
        scale = HD ** (-0.5)
        half = HD // 2
        qkv = (x @ Wqkv).reshape(B, T, 3, H, HD).transpose(2, 0, 3, 1, 4)
        q, k, v = (qkv[0], qkv[1], qkv[2])
        inv_freq = 1.0 / 10000.0 ** (jnp.arange(0, HD, 2, dtype=jnp.float32) / HD)
        t = jnp.arange(T, dtype=jnp.float32)
        freqs = jnp.outer(t, inv_freq)
        cos = jnp.cos(freqs)[None, None]
        sin = jnp.sin(freqs)[None, None]

        def rope(u):
            u1, u2 = (u[..., :half], u[..., half:])
            return jnp.concatenate([u1 * cos - u2 * sin, u1 * sin + u2 * cos], axis=-1)
        q = rope(q)
        k = rope(k)
        attn = jnp.einsum('bhqd,bhkd->bhqk', q, k) * scale
        i = jnp.arange(T)[:, None]
        j = jnp.arange(T)[None, :]
        mask = (j <= i) & (j > i - WIN)
        attn = jnp.where(mask[None, None], attn, -jnp.inf)
        attn = jax.nn.softmax(attn, axis=-1)
        out = jnp.einsum('bhqk,bhkd->bhqd', attn, v)
        out = out.transpose(0, 2, 1, 3).reshape(B, T, H * HD)
        return out @ Wout

    def _L0_xattn_ref(q, k, v, w_q, w_k, w_v, w_o):
        import math
        import jax, jax.numpy as jnp
        import numpy as np
        H = 16
        D_MODEL = 256
        D_K = 64
        D_V = 64
        b, n, _ = q.shape
        qh = (q @ w_q.T).reshape(b, n, H, D_K).transpose(0, 2, 1, 3)
        kh = (k @ w_k.T).reshape(b, n, H, D_K).transpose(0, 2, 1, 3)
        vh = (v @ w_v.T).reshape(b, n, H, D_V).transpose(0, 2, 1, 3)
        scores = jnp.einsum('bhid,bhjd->bhij', qh, kh) / math.sqrt(D_K)
        causal = jnp.tril(jnp.ones((n, n), dtype=bool))
        scores = jnp.where(causal[None, None], scores, -jnp.inf)
        attn = jax.nn.softmax(scores, axis=-1)
        out = jnp.einsum('bhij,bhjd->bhid', attn, vh)
        out = out.transpose(0, 2, 1, 3).reshape(b, n, H * D_V)
        return out @ w_o.T

    def _L0_ffn_ref(x, W_fc, ln_w, ln_b, W_proj):
        import jax, jax.numpy as jnp
        import numpy as np
        EPS = 1e-06
        LN_EPS = 1e-05

        def _absmean_core(W):
            gamma = jnp.mean(jnp.abs(W)) + EPS
            Ws = W / gamma
            Wq = jnp.sign(Ws) * jnp.minimum(jnp.round(jnp.abs(Ws)), 1.0)
            return (Wq, gamma)

        @jax.custom_vjp
        def absmean(W):
            return _absmean_core(W)[0]

        def _absmean_fwd(W):
            Wq, gamma = _absmean_core(W)
            return (Wq, gamma)

        def _absmean_bwd(gamma, g):
            return (g / gamma,)
        absmean.defvjp(_absmean_fwd, _absmean_bwd)

        def layernorm(x, w, b, eps=LN_EPS):
            mu = jnp.mean(x, axis=-1, keepdims=True)
            var = jnp.mean((x - mu) ** 2, axis=-1, keepdims=True)
            return (x - mu) * jax.lax.rsqrt(var + eps) * w + b
        h = jnp.einsum('btd,hd->bth', x, absmean(W_fc))
        h = jax.nn.gelu(h, approximate=False)
        h = layernorm(h, ln_w, ln_b)
        return jnp.einsum('bth,dh->btd', h, absmean(W_proj))
    x = x + _L0_attn_ref(_layernorm(x, axis=-1), L0_attn_Wqkv, L0_attn_Wout)
    x = x + _L0_xattn_ref(_layernorm(x, axis=-1), ctx_1024, ctx_1024, L0_xattn_w_q, L0_xattn_w_k, L0_xattn_w_v, L0_xattn_w_o)
    x = x + _L0_ffn_ref(_layernorm(x, axis=-1), L0_ffn_W_fc, L0_ffn_ln_w, L0_ffn_ln_b, L0_ffn_W_proj)
    return x

_drawn_inputs = setup_inputs


def setup_inputs(seed=0):
    import zlib

    import numpy as np

    out = dict(_drawn_inputs(seed))
    spreads = {'L0_ffn_ln_w': (1.0, 0.2), 'L0_ffn_ln_b': (0.0, 0.1)}
    factors = {}
    for name, (base, spread) in spreads.items():
        noise = np.random.default_rng([zlib.crc32(name.encode()), seed]).standard_normal(out[name].shape)
        drawn = base * np.exp(spread * noise) if base else spread * noise
        out[name] = jnp.asarray(drawn.astype(out[name].dtype))
    for name, factor in factors.items():
        out[name] = (out[name] * factor).astype(out[name].dtype)
    return out
```

```python
from contextlib import ExitStack

import concourse.bass as bass
from concourse import mybir

F32 = mybir.dt.float32
F32R = mybir.dt.float32r
BF16 = mybir.dt.bfloat16
ALU = mybir.AluOpType
ACT = mybir.ActivationFunctionType
AX_X = mybir.AxisListType.X

P = 128
B, T, D = 16, 128, 256
NB = 2
G = B // NB
GT = NB * T
DC = D // P
HD = 64
H1 = 8
H2 = 16
I1 = H1 * HD
I2 = H2 * HD
F = 1024
FC = F // P
TH = 4
T1 = NB * H1 // TH
T2 = NB * H2 // TH
WP = 8
SCALE = HD ** -0.5
LN_EPS = 1e-5
GAMMA_EPS = 1e-6


class Phase:

    def __init__(self, sem, tag, units, tiles=0):
        self.U = units
        self.T = tiles
        self.half = tiles // NB
        self.stats_done = sem(tag + "_stats_done")
        self.aggr_done = sem(tag + "_aggr_done")
        self.vareps_done = sem(tag + "_vareps_done")
        self.rstd_ready = sem(tag + "_rstd_ready")
        self.xn_ready = sem(tag + "_xn_ready")
        self.lnt_done = sem(tag + "_lnt_done")
        self.xh_ready = sem(tag + "_xh_ready")
        self.xl_ready = sem(tag + "_xl_ready")
        self.pj_ready = sem(tag + "_pj_ready")
        self.out_ready = sem(tag + "_out_ready")
        self.resid_done = sem(tag + "_resid_done")


class AttentionPhase(Phase):
    def __init__(self, sem, tag, units, tiles):
        super().__init__(sem, tag, units, tiles)
        self.s_ready = sem(tag + "_s_ready")
        self.maxed = sem(tag + "_maxed")
        self.subbed = sem(tag + "_subbed")
        self.exped = sem(tag + "_exped")
        self.summed = sem(tag + "_summed")
        self.rc_ready = sem(tag + "_rc_ready")
        self.normed = sem(tag + "_normed")
        self.transposed = sem(tag + "_transposed")
        self.pt_ready = sem(tag + "_pt_ready")
        self.av_done = sem(tag + "_av_done")
        self.oh_ready = sem(tag + "_oh_ready")
        self.ol_ready = sem(tag + "_ol_ready")
        self.v_ready = sem(tag + "_v_ready")


class SelfPhase(AttentionPhase):
    def __init__(self, sem, tag, units, tiles):
        super().__init__(sem, tag, units, tiles)
        self.roped = sem(tag + "_roped")
        self.k_step = sem(tag + "_k_step")
        self.qk_ready = sem(tag + "_qk_ready")


class CrossPhase(AttentionPhase):
    def __init__(self, sem, tag, units, tiles):
        super().__init__(sem, tag, units, tiles)
        self.ch_done = sem(tag + "_ch_done")
        self.cl_ready = sem(tag + "_cl_ready")
        self.q_ready = sem(tag + "_q_ready")
        self.ka_ready = sem(tag + "_ka_ready")
        self.kd_ready = sem(tag + "_kd_ready")


class FfnPhase(Phase):
    def __init__(self, sem, tag, units):
        super().__init__(sem, tag, units)
        self.g_ready = sem(tag + "_g_ready")
        self.gstats_done = sem(tag + "_gstats_done")
        self.gaggr_done = sem(tag + "_gaggr_done")
        self.gvareps_done = sem(tag + "_gvareps_done")
        self.grstd_ready = sem(tag + "_grstd_ready")
        self.gscaled = sem(tag + "_gscaled")
        self.gn_ready = sem(tag + "_gn_ready")
        self.gt_ready = sem(tag + "_gt_ready")
        self.hh_ready = sem(tag + "_hh_ready")
        self.hl_ready = sem(tag + "_hl_ready")


def decoder_program(nc, x_d, ctxT_d, wqkv_d, wout_d, wx_d, wfcT_d, wprojT_d, lnw_d, lnb_d, const_d, out_d):
    with ExitStack() as ctx:
        nxt = [nc.sbuf_base + (-nc.sbuf_base) % 32]

        def region(nbytes):
            at = nxt[0]
            nxt[0] = at + nbytes
            return at

        def sb(name, shape, dt=F32, at=None):
            n = 2 if dt == BF16 else 4
            for s in shape[1:]:
                n *= s
            if at is None:
                at = region(n + (-n) % 32)
            return nc.alloc_sbuf_tensor_at(name, shape, dt, offset=at)

        def sem(name):
            return ctx.enter_context(nc.semaphore(name))

        x_sb = sb("x_sb", [P, B, D])
        const = sb("const", [P, 5, P])
        cos_t, sin_t, ident = const[:, 0, :], const[:, 1, :], const[:, 2, :]
        mask_w = sb("mask_w", [P, TH, P], BF16)
        mask_c = sb("mask_c", [P, TH, P], BF16)
        ident_b = sb("ident_b", [P, P], BF16)
        ones_t = sb("ones_t", [P, P])
        lnw_bc = sb("lnw_bc", [P, F])
        lnb_bc = sb("lnb_bc", [P, F])
        xn = sb("xn", [P, NB, D])
        xh = sb("xh", [P, DC, GT], F32R)
        xl = sb("xl", [P, DC, GT], F32R)
        stats = sb("stats", [P, NB, 6])
        mv = sb("mv", [P, NB, 2])
        vareps = sb("vareps", [P, NB])
        rstd = sb("rstd", [P, NB])
        scratch = sb("scratch", [P, 1])
        neghalf = sb("neghalf", [P, NB])
        mx = sb("mx", [P, 4, TH])
        sm = sb("sm", [P, 4, TH])
        rc = sb("rc", [P, 4, TH])
        prob = sb("prob", [P, 4, TH * P])
        probT = sb("probT", [P, 2, TH * P])
        oh = sb("oh", [P, NB, H2 // 2, P], F32R)
        ol = sb("ol", [P, NB, H2 // 2, P], F32R)
        stage = sb("stage", [P, F])
        gstats = sb("gstats", [P, NB, 2, 6])
        gmv = sb("gmv", [P, NB, 2])
        gvareps = sb("gvareps", [P, NB])
        grstd = sb("grstd", [P, NB])
        asum = sb("asum", [P, 4])
        gam = sb("gam", [P, 2])
        thr = sb("thr", [P, 2])
        nthr = sb("nthr", [P, 2])

        r_q = region(H2 // 2 * GT * 4)
        qA = sb("qA", [P, 2, 2, GT], at=r_q)
        qB = sb("qB", [P, H2 // 2, GT], at=r_q)
        r_k = region(16384)
        kA = sb("kA", [P, 2, 2, NB, TH, P], at=r_k)
        kB = sb("kB", [P, H2 // 2, NB, 2, P], at=r_k)
        hTh = sb("hTh", [P, NB, FC, P], F32R, at=r_k)
        hTl = sb("hTl", [P, NB, FC, P], F32R, at=r_k + 8192)
        r_v = region(8192)
        vA = sb("vA", [P, NB, I1], at=r_v)
        vB = sb("vB", [P, NB, I2], at=r_v)
        g = sb("g", [P, NB, F], at=r_v)
        r_m = region(8192)
        ropec = sb("ropec", [P, 2, 2, GT], at=r_m)
        ropes = sb("ropes", [P, 2, 2, GT], at=r_m + 4096)
        craw = sb("craw", [P, DC, GT], at=r_m)
        ch = sb("ch", [P, DC, GT], F32R, at=r_m + 2048)
        cl = sb("cl", [P, DC, GT], F32R, at=r_m + 4096)
        r_1 = region(32768)
        w1h = sb("w1h", [P, DC, 3 * I1], F32R, at=r_1)
        w1l = sb("w1l", [P, DC, 3 * I1], F32R, at=r_1 + 12288)
        woh = sb("woh", [P, I1 // P, D], F32R, at=r_1 + 24576)
        wol = sb("wol", [P, I1 // P, D], F32R, at=r_1 + 28672)
        fraw = sb("fraw", [P, 2, DC * F], at=r_1)
        wfc = sb("wfc", [P, DC, F], F32R, at=r_1 + 16384)
        wpj = sb("wpj", [P, FC, D], F32R, at=r_1 + 24576)
        r_2 = region(65536)
        w1raw = sb("w1raw", [P, DC, 3 * I1], at=r_2)
        woraw = sb("woraw", [P, I1 // P, D], at=r_2 + 12288)
        w2 = sb("w2", [P, 2, WP, F], F32R, at=r_2)
        assert nxt[0] <= nc.sbuf_usable_end, nxt[0]

        def ps(name):
            return ctx.enter_context(nc.psum_tensor(name, [P, 512], F32))
        ps_s = [ps("ps_s0"), ps("ps_s1")]
        ps_t = ps("ps_t")
        ps_p = [ps("ps_p0"), ps("ps_p1")]
        ps_o = [ps("ps_o0"), ps("ps_o1")]
        ps_x = ps("ps_x")

        ld_x0, ld_xr, ld_c, ld_w1, ld_wo, ld_ln = (sem(n) for n in ("ld_x0", "ld_xr", "ld_c", "ld_w1", "ld_wo", "ld_ln"))
        ld_w2, ld_ctx, ld_f, st_out = (sem(n) for n in ("ld_w2", "ld_ctx", "ld_f", "st_out"))
        masks_ready, k_zeroed, kB_zeroed, ones_ready = (sem(n) for n in ("masks_ready", "k_zeroed", "kB_zeroed", "ones_ready"))
        w1h_ready, w1l_ready, wo_ready, woh_done = (sem(n) for n in ("w1h_ready", "w1l_ready", "wo_ready", "woh_done"))
        w2_hi, w2_ready = sem("w2_hi"), sem("w2_ready")
        abs_summed, gam_summed, thr_step, tern_neg, tern_ready = (
            sem(n) for n in ("abs_summed", "gam_summed", "thr_step", "tern_neg", "tern_ready"))

        A = SelfPhase(sem, "a", 6, T1)
        X = CrossPhase(sem, "b", 12, T2)
        C = FfnPhase(sem, "c", 4)

        def bcast(ap, n):
            return ap.unsqueeze(2).to_broadcast([P, ap.shape[1], n])

        def f32(ap):
            return ap.bitcast(F32)

        def wait_if(engine, semaphore, value):
            if not isinstance(value, int) or value > 0:
                engine.wait_ge(semaphore, value)

        block = ctx.enter_context(nc.Block())

        @block.sync
        def _(sp):
            x_v = x_d.rearrange("(b t) d -> t b d", t=T)
            sp.dma_start(x_sb[:, 0:NB, :], x_v[:, 0:NB, :]).then_inc(ld_x0, 16)
            sp.dma_start(w1raw[:, :, :], wqkv_d.rearrange("(c p) n -> p c n", p=P)).then_inc(ld_w1, 16)
            sp.dma_start(const[:, :, :], const_d.rearrange("p (k n) -> p k n", k=5)).then_inc(ld_c, 16)
            sp.dma_start(woraw[:, :, :], wout_d.rearrange("(c p) n -> p c n", p=P)).then_inc(ld_wo, 16)
            sp.dma_start(x_sb[:, NB:B, :], x_v[:, NB:B, :]).then_inc(ld_xr, 16)
            sp.dma_start(lnw_bc[:, :], lnw_d.partition_broadcast(P)).then_inc(ld_ln, 16)
            sp.dma_start(lnb_bc[:, :], lnb_d.partition_broadcast(P)).then_inc(ld_ln, 16)

            def w2_load(i):
                wait_if(sp, w2_ready, i)
                sp.dma_start(stage[:, :], wx_d[bass.ds(i, 1), :, :].rearrange("a p n -> p (a n)")).then_inc(ld_w2, 16)
            w2_load(0)
            with sp.Fori(1, WP) as i:
                w2_load(i)

            ctx_v = ctxT_d.rearrange("(c p) n -> p c n", p=P)

            def ctx_load(n):
                wait_if(sp, X.cl_ready, n)
                sp.dma_start(craw[:, :, :], ctx_v[:, :, bass.ds(n * GT, GT)]).then_inc(ld_ctx, 16)
            sp.wait_ge(A.qk_ready, 4 * G)
            ctx_load(0)
            sp.wait_ge(A.out_ready, NB * G)
            sp.dma_start(fraw[:, 0, :].rearrange("p (c n) -> p c n", c=DC),
                         wfcT_d.rearrange("(c p) n -> p c n", p=P)).then_inc(ld_f, 16)
            sp.dma_start(fraw[:, 1, :].rearrange("p (c n) -> p c n", c=FC),
                         wprojT_d.rearrange("(c p) n -> p c n", p=P)).then_inc(ld_f, 16)
            with sp.Fori(1, G) as n:
                ctx_load(n)

            out_v = out_d.rearrange("(b t) d -> t b d", t=T)
            with sp.Fori(0, G) as i:
                sp.wait_ge(C.resid_done, i + 1)
                sp.dma_start(out_v[:, bass.ds(NB * i, NB), :], x_sb[:, bass.ds(NB * i, NB), :]).then_inc(st_out, 16)
            sp.wait_ge(st_out, 16 * G)

        @block.tensor
        def _(pe):
            mm = nc.tensor.matmul

            def product(out, lh, ll, rh, rl, first, last):
                mm(out, lh, rh, start=first, stop=False)
                mm(out, lh, rl, start=False, stop=False)
                return mm(out, ll, rh, start=False, stop=last)

            def ln_transposes(ph, n):
                pe.wait_ge(ph.xn_ready, n + 1)
                for b in range(NB):
                    for c in range(DC):
                        last = nc.tensor.transpose(ps_x[:, c * GT + b * T:c * GT + (b + 1) * T],
                                                   xn[:, b, c * P:(c + 1) * P], ident)
                last.then_inc(ph.lnt_done, 1)

            def unit_bank(freed, n, u):
                done, per_group, count = freed[u]
                wait_if(pe, done, n * per_group + count)
                return ps_p[u % 2]

            a_freed = [(A.roped, 4, 0), (A.v_ready, 2, 0), (A.roped, 4, 1), (A.roped, 4, 2), (A.roped, 4, 3),
                       (A.v_ready, 2, 1)]
            x_freed = [(X.v_ready, 4, 0), (X.v_ready, 4, 0), (X.v_ready, 4, 1), (X.v_ready, 4, 2),
                       (X.q_ready, 4, 1), (X.q_ready, 4, 2), (X.q_ready, 4, 3), (X.q_ready, 4, 4),
                       (X.ka_ready, 2, 1), (X.ka_ready, 2, 2), (X.kd_ready, 2, 1), (X.kd_ready, 2, 2)]
            c_freed = [(C.g_ready, 4, 0), (C.g_ready, 4, 0), (C.g_ready, 4, 1), (C.g_ready, 4, 2)]

            def tr(ph, i, t):
                pe.wait_ge(ph.normed, i * ph.T + t + 1)
                wait_if(pe, ph.pt_ready, i * ph.T + t)
                for h in range(TH):
                    last = nc.tensor.transpose(ps_t[:, h * P:(h + 1) * P],
                                               prob[:, t % 4, h * P:(h + 1) * P], ident)
                last.then_inc(ph.transposed, 1)

            def av(ph, i, t, v):
                pe.wait_ge(ph.pt_ready, i * ph.T + t + 1)
                wait_if(pe, ph.ol_ready, i * ph.T + max(t - 1, 0))
                b, q = t // ph.half, t % ph.half
                for h in range(TH):
                    head, col = q * TH + h, (h // 2) * P
                    last = mm(ps_o[t % 2][HD * (h % 2):HD * (h % 2 + 1), col:col + P],
                              v[:, b, head * HD:(head + 1) * HD], probT[:, t % 2, h * P:(h + 1) * P],
                              start=True, stop=True)
                last.then_inc(ph.av_done, 1)

            def project_out(ph, i, b, wh, wl, nj):
                pe.wait_ge(ph.ol_ready, i * ph.T + (b + 1) * ph.half)
                for j in range(nj):
                    last = product(ps_x[:, b * D:(b + 1) * D], oh[:, b, j, :], ol[:, b, j, :], wh(j), wl(j),
                                   j == 0, j == nj - 1)
                last.then_inc(ph.out_ready, 1)

            def a_lnt(n):
                if not isinstance(n, int) or n >= 2:
                    wait_if(pe, A.resid_done, n - 1)
                ln_transposes(A, n)

            def a_qk(n, c, u):
                bank = unit_bank(a_freed, n, u)
                pe.wait_ge(A.xl_ready, n + 1)
                for ab in range(2):
                    col = (2 * c + ab) * P
                    for d in range(DC):
                        last = product(bank[:, ab * GT:(ab + 1) * GT], w1h[:, d, col:col + P], w1l[:, d, col:col + P],
                                       xh[:, d, :], xl[:, d, :], d == 0, d == DC - 1)
                last.then_inc(A.pj_ready, 1)

            def a_v(n, b, u):
                bank = unit_bank(a_freed, n, u)
                for d in range(DC):
                    last = product(bank[:, :], xh[:, d, b * T:(b + 1) * T], xl[:, d, b * T:(b + 1) * T],
                                   w1h[:, d, 2 * I1:], w1l[:, d, 2 * I1:], d == 0, d == DC - 1)
                last.then_inc(A.pj_ready, 1)

            def a_s(i, t):
                b, hg = t // A.half, t % A.half
                wait_if(pe, A.subbed, i * T1 + max(t - 1, 0))
                pe.wait_ge(A.qk_ready, 4 * i + 4)
                mm(ps_s[t % 2][:, :], ident_b[:, :], mask_w[:, :, :], start=True, stop=False)
                for ab in range(2):
                    last = mm(ps_s[t % 2][:, :], qA[:, hg, ab, b * T:(b + 1) * T], kA[:, hg, ab, b, :, :],
                              start=False, stop=ab == 1)
                last.then_inc(A.s_ready, 1)

            def a_out(i, b):
                project_out(A, i, b, lambda j: woh[:, j, :], lambda j: wol[:, j, :], I1 // P)

            pe.wait_ge(ld_c, 16)
            a_lnt(0)
            pe.wait_ge(w1h_ready, 1)
            pe.wait_ge(w1l_ready, 1)
            for u, c in ((0, 0), (1, 1), (2, 2)):
                a_qk(0, c, u)
            a_v(0, 0, 3)
            a_qk(0, 3, 4)
            a_v(0, 1, 5)
            pe.wait_ge(masks_ready, 3)
            pe.wait_ge(wo_ready, 1)

            def a_step(i, n):
                a_s(i, 0)
                a_s(i, 1)
                if n is not None:
                    a_lnt(n)
                a_s(i, 2)
                a_s(i, 3)
                if n is not None:
                    a_qk(n, 0, 0)
                tr(A, i, 0)
                if n is not None:
                    a_qk(n, 1, 1)
                tr(A, i, 1)
                pe.wait_ge(A.v_ready, NB * i + NB)
                av(A, i, 0, vA)
                if n is not None:
                    a_qk(n, 2, 2)
                tr(A, i, 2)
                av(A, i, 1, vA)
                if n is not None:
                    a_v(n, 0, 3)
                    a_qk(n, 3, 4)
                tr(A, i, 3)
                av(A, i, 2, vA)
                av(A, i, 3, vA)
                if n is not None:
                    a_v(n, 1, 5)
                    pe.wait_ge(A.xl_ready, n + 1)
                a_out(i, 0)
                a_out(i, 1)
            a_step(0, 1)
            with pe.Fori(1, G - 1) as i:
                a_step(i, i + 1)
            a_step(G - 1, None)

            def wx(k, piece, lo, hi):
                return w2[:, k, piece, lo:hi]

            def b_lnt(n):
                if isinstance(n, int) and n == 0:
                    pe.wait_ge(A.resid_done, G)
                else:
                    wait_if(pe, X.resid_done, n - 1)
                ln_transposes(X, n)

            def b_pairs(n, c, u, base, src_h, src_l, ready):
                bank = unit_bank(x_freed, n, u)
                pe.wait_ge(ready, n + 1)
                for s in range(2):
                    col = (2 * c + s) * P
                    for d in range(DC):
                        last = product(bank[:, s * GT:(s + 1) * GT], wx(0, base + d, col, col + P),
                                       wx(1, base + d, col, col + P), src_h[:, d, :], src_l[:, d, :],
                                       d == 0, d == DC - 1)
                last.then_inc(X.pj_ready, 1)

            def b_q(n, c, u):
                b_pairs(n, c, u, 0, xh, xl, X.xl_ready)

            def b_k(n, c, u):
                b_pairs(n, c, u, 2, ch, cl, X.cl_ready)

            def b_v(n, b, s, u):
                bank = unit_bank(x_freed, n, u)
                pe.wait_ge(X.cl_ready, n + 1)
                for d in range(DC):
                    last = product(bank[:, :], ch[:, d, b * T:(b + 1) * T], cl[:, d, b * T:(b + 1) * T],
                                   wx(0, 4 + d, s * 512, s * 512 + 512), wx(1, 4 + d, s * 512, s * 512 + 512),
                                   d == 0, d == DC - 1)
                last.then_inc(X.pj_ready, 1)

            def b_s(i, t):
                b, q = t // X.half, t % X.half
                wait_if(pe, X.subbed, i * T2 + max(t - 1, 0))
                pe.wait_ge(X.q_ready, 4 * i + 4)
                pe.wait_ge(X.ka_ready, 2 * i + 2)
                pe.wait_ge(X.kd_ready, 2 * i + 2)
                mm(ps_s[t % 2][:, :], ident_b[:, :], mask_c[:, :, :], start=True, stop=False)
                for s in range(2):
                    pair = 2 * q + s
                    last = mm(ps_s[t % 2][:, s * 2 * P:(s + 1) * 2 * P], qB[:, pair, b * T:(b + 1) * T],
                              kB[:, pair, b, :, :], start=False, stop=s == 1)
                last.then_inc(X.s_ready, 1)

            def b_out(i, b):
                project_out(X, i, b, lambda j: wx(0, 6 + j // 4, j % 4 * D, j % 4 * D + D),
                            lambda j: wx(1, 6 + j // 4, j % 4 * D, j % 4 * D + D), I2 // P)

            pe.wait_ge(w2_ready, WP)
            b_lnt(0)
            b_v(0, 0, 0, 0)
            b_v(0, 0, 1, 1)
            for c in range(4):
                b_q(0, c, 2 + c)
            for c in range(4):
                b_k(0, c, 6 + c)
            b_v(0, 1, 0, 10)
            b_v(0, 1, 1, 11)

            def gamma_total():
                pe.wait_ge(abs_summed, 4)
                pe.wait_ge(ones_ready, 1)
                mm(ps_x[:, 0:4], ones_t[:, :], asum[:, :], start=True, stop=True).then_inc(gam_summed, 1)

            def b_step(i, n):
                b_s(i, 0)
                b_s(i, 1)
                if n is not None:
                    b_lnt(n)
                else:
                    pe.wait_ge(X.resid_done, G - 1)
                    gamma_total()
                b_s(i, 2)
                b_s(i, 3)
                pe.wait_ge(X.v_ready, 4 * i + 4)
                for t in range(4):
                    tr(X, i, t)
                    b_s(i, t + 4)
                    if t:
                        av(X, i, t - 1, vB)
                tr(X, i, 4)
                av(X, i, 3, vB)
                if n is not None:
                    b_v(n, 0, 0, 0)
                    b_v(n, 0, 1, 1)
                tr(X, i, 5)
                av(X, i, 4, vB)
                if n is not None:
                    b_q(n, 0, 2)
                    b_q(n, 1, 3)
                tr(X, i, 6)
                av(X, i, 5, vB)
                if n is not None:
                    b_q(n, 2, 4)
                    b_q(n, 3, 5)
                    pe.wait_ge(X.xl_ready, n + 1)
                else:
                    pe.wait_ge(thr_step, 1)
                b_out(i, 0)
                tr(X, i, 7)
                av(X, i, 6, vB)
                if n is not None:
                    b_k(n, 0, 6)
                    b_k(n, 1, 7)
                av(X, i, 7, vB)
                if n is not None:
                    b_k(n, 2, 8)
                    b_k(n, 3, 9)
                    b_v(n, 1, 0, 10)
                    b_v(n, 1, 1, 11)
                b_out(i, 1)
            b_step(0, 1)
            with pe.Fori(1, G - 1) as i:
                b_step(i, i + 1)
            b_step(G - 1, None)

            def c_fc(n, b, s):
                u = 2 * b + s
                bank = unit_bank(c_freed, n, u)
                pe.wait_ge(C.xl_ready, n + 1)
                for d in range(DC):
                    w = wfc[:, d, s * 512:(s + 1) * 512]
                    mm(bank[:, :], xh[:, d, b * T:(b + 1) * T], w, start=d == 0, stop=False)
                    last = mm(bank[:, :], xl[:, d, b * T:(b + 1) * T], w, start=False, stop=d == DC - 1)
                last.then_inc(C.pj_ready, 1)

            def c_tr(i, b):
                pe.wait_ge(C.gn_ready, NB * i + b + 1)
                wait_if(pe, C.hl_ready, 2 * (NB * i + b))
                for j in range(FC):
                    last = nc.tensor.transpose(ps_s[j // 4][:, j % 4 * P:(j % 4 + 1) * P],
                                               g[:, b, j * P:(j + 1) * P], ident)
                last.then_inc(C.gt_ready, 1)

            def c_out(i, b):
                pe.wait_ge(C.hl_ready, 2 * (NB * i + b + 1))
                wait_if(pe, C.resid_done, i)
                for j in range(FC):
                    mm(ps_o[0][:, b * D:(b + 1) * D], hTh[:, b, j, :], wpj[:, j, :], start=j == 0, stop=False)
                    last = mm(ps_o[0][:, b * D:(b + 1) * D], hTl[:, b, j, :], wpj[:, j, :], start=False, stop=j == FC - 1)
                last.then_inc(C.out_ready, 1)

            def c_lnt(n):
                if isinstance(n, int) and n == 0:
                    pe.wait_ge(X.resid_done, G)
                else:
                    wait_if(pe, C.xl_ready, n)
                ln_transposes(C, n)

            c_lnt(0)
            pe.wait_ge(tern_ready, 4)
            for b in range(NB):
                for s in range(2):
                    c_fc(0, b, s)

            def c_step(i, n):
                if n is not None:
                    c_lnt(n)
                c_tr(i, 0)
                if n is not None:
                    c_fc(n, 0, 0)
                    c_fc(n, 0, 1)
                c_tr(i, 1)
                c_out(i, 0)
                if n is not None:
                    c_fc(n, 1, 0)
                    c_fc(n, 1, 1)
                c_out(i, 1)
            c_step(0, 1)
            with pe.Fori(1, G - 1) as i:
                c_step(i, i + 1)
            c_step(G - 1, None)

        @block.scalar
        def _(act):
            def copy(out, in_):
                return nc.scalar.activation(out, in_, ACT.Copy)

            def x_hi(ph, n):
                act.wait_ge(ph.lnt_done, n + 1)
                wait_if(act, ph.pj_ready, n * ph.U)
                copy(xh[:, :, :], ps_x[:, :].rearrange("p (c n) -> p c n", c=DC)).then_inc(ph.xh_ready, 1)

            def exp(ph, i, t):
                act.wait_ge(ph.subbed, i * ph.T + t + 1)
                nc.scalar.activation(prob[:, t % 4, :], prob[:, t % 4, :], ACT.Exp, scale=SCALE).then_inc(ph.exped, 1)

            def pt_copy(ph, i, t):
                act.wait_ge(ph.transposed, i * ph.T + t + 1)
                wait_if(act, ph.av_done, i * ph.T + max(t - 1, 0))
                copy(probT[:, t % 2, :], ps_t[:, :]).then_inc(ph.pt_ready, 1)

            def o_hi(ph, i, t):
                b, q = t // ph.half, t % ph.half
                act.wait_ge(ph.av_done, i * ph.T + t + 1)
                wait_if(act, ph.out_ready, NB * i)
                copy(oh[:, b, 2 * q:2 * q + 2, :],
                     ps_o[t % 2][:, 0:2 * P].rearrange("p (j n) -> p j n", j=2)
                     ).then_inc(ph.oh_ready, 1)

            def a_v(n, b, u):
                act.wait_ge(A.pj_ready, n * A.U + u + 1)
                if not (isinstance(n, int) and n == 0):
                    act.wait_ge(A.av_done, (n - 1) * T1 + (b + 1) * A.half)
                copy(vA[:, b, :], ps_p[u % 2][:, :]).then_inc(A.v_ready, 1)

            act.wait_ge(ld_w1, 16)
            copy(w1h[:, :, :], w1raw[:, :, :]).then_inc(w1h_ready, 1)
            x_hi(A, 0)
            a_v(0, 0, 3)
            a_v(0, 1, 5)

            def a_step(i, n):
                exp(A, i, 0)
                exp(A, i, 1)
                if n is not None:
                    x_hi(A, n)
                exp(A, i, 2)
                exp(A, i, 3)
                pt_copy(A, i, 0)
                pt_copy(A, i, 1)
                o_hi(A, i, 0)
                pt_copy(A, i, 2)
                o_hi(A, i, 1)
                if n is not None:
                    a_v(n, 0, 3)
                pt_copy(A, i, 3)
                o_hi(A, i, 2)
                o_hi(A, i, 3)
                if n is not None:
                    a_v(n, 1, 5)
            a_step(0, 1)
            with act.Fori(1, G - 1) as i:
                a_step(i, i + 1)
            a_step(G - 1, None)

            def ctx_hi(n):
                act.wait_ge(ld_ctx, 16 * (n + 1))
                wait_if(act, X.pj_ready, n * X.U)
                copy(ch[:, :, :], craw[:, :, :]).then_inc(X.ch_done, 1)

            def b_v(n, b, s, u):
                act.wait_ge(X.pj_ready, n * X.U + u + 1)
                if isinstance(n, int) and n == 0:
                    act.wait_ge(A.av_done, T1 * G)
                else:
                    act.wait_ge(X.av_done, (n - 1) * T2 + (b + 1) * X.half)
                copy(vB[:, b, s * 512:(s + 1) * 512], ps_p[u % 2][:, :]).then_inc(X.v_ready, 1)

            def b_q(n, c, u):
                act.wait_ge(X.pj_ready, n * X.U + u + 1)
                wait_if(act, X.s_ready, n * T2)
                copy(qB[:, 2 * c:2 * c + 2, :], ps_p[u % 2][:, :].rearrange("p (j n) -> p j n", j=2)
                     ).then_inc(X.q_ready, 1)

            def b_k(n, c, u):
                act.wait_ge(X.pj_ready, n * X.U + u + 1)
                wait_if(act, X.s_ready, n * T2)
                for h in range(2):
                    r = slice(HD * h, HD * h + HD)
                    last = copy(kB[r, 2 * c:2 * c + 2, :, h, :],
                                ps_p[u % 2][r, :].rearrange("p (j b n) -> p j b n", j=2, b=NB))
                last.then_inc(X.ka_ready, 1)

            ctx_hi(0)
            x_hi(X, 0)
            b_v(0, 0, 0, 0)
            b_v(0, 0, 1, 1)
            for c in range(4):
                b_q(0, c, 2 + c)
            act.wait_ge(kB_zeroed, 2)
            b_k(0, 0, 6)
            b_k(0, 1, 7)
            b_v(0, 1, 0, 10)
            b_v(0, 1, 1, 11)

            def abs_sums():
                act.wait_ge(ld_f, 32)
                for k in range(4):
                    if k:
                        act.wait_ge(abs_summed, k)
                    nc.scalar.activation(stage[:, :], fraw[:, k // 2, k % 2 * F:(k % 2 + 1) * F], ACT.Abs,
                                         accum_out=asum[:, k:k + 1]).then_inc(abs_summed, 1)

            def b_step(i, n):
                if n is None:
                    abs_sums()
                exp(X, i, 0)
                exp(X, i, 1)
                if n is not None:
                    x_hi(X, n)
                    ctx_hi(n)
                exp(X, i, 2)
                exp(X, i, 3)
                pt_copy(X, i, 0)
                for t in range(3):
                    exp(X, i, t + 4)
                    pt_copy(X, i, t + 1)
                    o_hi(X, i, t)
                exp(X, i, 7)
                pt_copy(X, i, 4)
                o_hi(X, i, 3)
                if n is not None:
                    b_v(n, 0, 0, 0)
                    b_v(n, 0, 1, 1)
                pt_copy(X, i, 5)
                o_hi(X, i, 4)
                if n is not None:
                    b_q(n, 0, 2)
                    b_q(n, 1, 3)
                pt_copy(X, i, 6)
                o_hi(X, i, 5)
                if n is not None:
                    b_q(n, 2, 4)
                    b_q(n, 3, 5)
                pt_copy(X, i, 7)
                o_hi(X, i, 6)
                if n is not None:
                    b_k(n, 0, 6)
                    b_k(n, 1, 7)
                o_hi(X, i, 7)
                if n is not None:
                    b_v(n, 1, 0, 10)
                    b_v(n, 1, 1, 11)
            b_step(0, 1)
            with act.Fori(1, G - 1) as i:
                b_step(i, i + 1)
            b_step(G - 1, None)

            def c_gelu(n, b):
                for s in range(2):
                    u = 2 * b + s
                    act.wait_ge(C.pj_ready, n * C.U + u + 1)
                    if isinstance(n, int) and n == 0:
                        act.wait_ge(X.av_done, T2 * G)
                    else:
                        act.wait_ge(C.gt_ready, NB * (n - 1) + b + 1)
                    nc.scalar.activation(g[:, b, s * 512:(s + 1) * 512], ps_p[u % 2][:, :], ACT.Gelu
                                         ).then_inc(C.g_ready, 1)

            def c_hi(i, b):
                act.wait_ge(C.gt_ready, NB * i + b + 1)
                act.wait_ge(C.out_ready, max(i - 1, 0) * NB + b + 1 if isinstance(i, int) else (i - 1) * NB + b + 1
                            ) if not (isinstance(i, int) and i == 0) else act.wait_ge(X.s_ready, T2 * G)
                for s in range(2):
                    copy(hTh[:, b, 4 * s:4 * s + 4, :], ps_s[s][:, :].rearrange("p (j n) -> p j n", j=4)
                         ).then_inc(C.hh_ready, 1)

            x_hi(C, 0)
            c_gelu(0, 0)
            c_gelu(0, 1)

            def c_step(i, n):
                if n is not None:
                    x_hi(C, n)
                c_hi(i, 0)
                if n is not None:
                    c_gelu(n, 0)
                c_hi(i, 1)
                if n is not None:
                    c_gelu(n, 1)
            c_step(0, 1)
            with act.Fori(1, G - 1) as i:
                c_step(i, i + 1)
            c_step(G - 1, None)

        @block.vector
        def _(dve):
            tt = nc.vector.tensor_tensor

            def x_stats(ph, n):
                for b in range(NB):
                    last = nc.vector.bn_stats(stats[:, b, :], x_sb[:, n * NB + b, :] if isinstance(n, int)
                                              else x_sb[:, bass.ds(n * NB + b, 1), :].rearrange("p a d -> p (a d)"))
                last.then_inc(ph.stats_done, 1)
                dve.wait_ge(ph.stats_done, n + 1)
                nc.vector.memset(scratch[:, :], 0.0)
                for b in range(NB):
                    last = nc.vector.bn_aggr(mv[:, b, :], stats[:, b, :])
                last.then_inc(ph.aggr_done, 1)
                dve.wait_ge(ph.aggr_done, n + 1)
                nc.vector.tensor_scalar(vareps[:, :], mv[:, :, 1], LN_EPS, None, ALU.add).then_inc(ph.vareps_done, 1)

            def x_norm(ph, n):
                dve.wait_ge(ph.rstd_ready, n + 1)
                wait_if(dve, ph.lnt_done, n)
                for b in range(NB):
                    last = nc.vector.tensor_scalar(
                        xn[:, b, :], x_sb[:, n * NB + b, :] if isinstance(n, int)
                        else x_sb[:, bass.ds(n * NB + b, 1), :].rearrange("p a d -> p (a d)"),
                        mv[:, b, 0:1], rstd[:, b:b + 1], ALU.subtract, ALU.mult)
                last.then_inc(ph.xn_ready, 1)

            def x_lo(ph, n):
                dve.wait_ge(ph.xh_ready, n + 1)
                tt(xl[:, :, :], ps_x[:, :].rearrange("p (c n) -> p c n", c=DC), f32(xh[:, :, :]), ALU.subtract
                   ).then_inc(ph.xl_ready, 1)

            def max_sub(ph, i, t):
                dve.wait_ge(ph.s_ready, i * ph.T + t + 1)
                s = ps_s[t % 2][:, :].rearrange("p (h k) -> p h k", h=TH)
                nc.vector.reduce_max(mx[:, t % 4, :], s, AX_X).then_inc(ph.maxed, 1)
                dve.wait_ge(ph.maxed, i * ph.T + t + 1)
                if t >= 4:
                    dve.wait_ge(ph.transposed, i * ph.T + t - 3)
                elif not (isinstance(i, int) and i == 0):
                    dve.wait_ge(ph.transposed, (i - 1) * ph.T + ph.T - 3 + t)
                tt(prob[:, t % 4, :].rearrange("p (h k) -> p h k", h=TH), s, bcast(mx[:, t % 4, :], P), ALU.subtract
                   ).then_inc(ph.subbed, 1)

            def row_sum(ph, i, t):
                dve.wait_ge(ph.exped, i * ph.T + t + 1)
                nc.vector.reduce_sum(sm[:, t % 4, :], prob[:, t % 4, :].rearrange("p (h k) -> p h k", h=TH), AX_X
                                     ).then_inc(ph.summed, 1)
                dve.wait_ge(ph.summed, i * ph.T + t + 1)
                nc.vector.reciprocal(rc[:, t % 4, :], sm[:, t % 4, :]).then_inc(ph.rc_ready, 1)

            def o_lo(ph, i, t):
                b, q = t // ph.half, t % ph.half
                dve.wait_ge(ph.oh_ready, i * ph.T + t + 1)
                tt(ol[:, b, 2 * q:2 * q + 2, :],
                   ps_o[t % 2][:, 0:2 * P].rearrange("p (j n) -> p j n", j=2),
                   f32(oh[:, b, 2 * q:2 * q + 2, :]), ALU.subtract).then_inc(ph.ol_ready, 1)

            def resid(ph, i, bank):
                dve.wait_ge(ph.out_ready, NB * i + NB)
                xs = x_sb[:, bass.ds(NB * i, NB), :]
                tt(xs, bank[:, :].rearrange("p (b d) -> p b d", b=NB), xs, ALU.add).then_inc(ph.resid_done, 1)

            def a_rope(n, c, u):
                dve.wait_ge(A.pj_ready, n * A.U + u + 1)
                if c >= 2:
                    wait_if(dve, A.qk_ready, n * 4 + c - 1)
                else:
                    wait_if(dve, A.qk_ready, n * 4)
                bank = ps_p[u % 2][:, :].rearrange("p (a n) -> p a n", n=P)
                for dst, tab in ((ropec, cos_t), (ropes, sin_t)):
                    last = tt(dst[:, c % 2, :, :].rearrange("p a (b n) -> p (a b) n", n=P), bank,
                              tab.unsqueeze(1).to_broadcast([P, 4, P]), ALU.mult)
                last.then_inc(A.roped, 1)

            dve.wait_ge(ld_x0, 16)
            x_stats(A, 0)
            dve.wait_ge(ld_c, 16)
            nc.vector.tensor_copy(ident_b[:, :], ident).then_inc(masks_ready, 1)
            for m, k in ((mask_w, 3), (mask_c, 4)):
                nc.vector.tensor_copy(m[:, :, :], const[:, k, :].unsqueeze(1).to_broadcast([P, TH, P])
                                      ).then_inc(masks_ready, 1)
            x_norm(A, 0)
            dve.wait_ge(w1h_ready, 1)
            tt(w1l[:, :, :], w1raw[:, :, :], f32(w1h[:, :, :]), ALU.subtract).then_inc(w1l_ready, 1)
            x_lo(A, 0)
            for c, u in ((0, 0), (1, 1), (2, 2), (3, 4)):
                a_rope(0, c, u)

            dve.wait_ge(ld_xr, 16)

            def a_step(i, n):
                if n is not None:
                    x_stats(A, n)
                max_sub(A, i, 0)
                if n is not None:
                    x_norm(A, n)
                max_sub(A, i, 1)
                row_sum(A, i, 0)
                if n is not None:
                    x_lo(A, n)
                max_sub(A, i, 2)
                row_sum(A, i, 1)
                max_sub(A, i, 3)
                row_sum(A, i, 2)
                if n is not None:
                    a_rope(n, 0, 0)
                row_sum(A, i, 3)
                if n is not None:
                    a_rope(n, 1, 1)
                o_lo(A, i, 0)
                if n is not None:
                    a_rope(n, 2, 2)
                o_lo(A, i, 1)
                if n is not None:
                    a_rope(n, 3, 4)
                o_lo(A, i, 2)
                o_lo(A, i, 3)
                resid(A, i, ps_x)
            a_step(0, 1)
            with dve.Fori(1, G - 1) as i:
                a_step(i, i + 1)
            a_step(G - 1, None)

            def b_k(n, c, u):
                dve.wait_ge(X.pj_ready, n * X.U + u + 1)
                wait_if(dve, X.s_ready, n * T2)
                for h in range(2):
                    r = slice(HD * h, HD * h + HD)
                    last = nc.vector.tensor_copy(kB[r, 2 * c:2 * c + 2, :, h, :],
                                                 ps_p[u % 2][r, :].rearrange("p (j b n) -> p j b n", j=2, b=NB))
                last.then_inc(X.kd_ready, 1)

            dve.wait_ge(A.resid_done, G)
            x_stats(X, 0)
            x_norm(X, 0)
            dve.wait_ge(A.s_ready, T1 * G)
            nc.vector.memset(kB[0:HD, :, :, 1, :].rearrange("p j b n -> p (j b) n"), 0.0).then_inc(kB_zeroed, 1)
            x_lo(X, 0)
            dve.wait_ge(kB_zeroed, 2)
            b_k(0, 2, 8)
            b_k(0, 3, 9)

            def ternarise():
                dve.wait_ge(gam_summed, 1)
                nc.vector.reduce_sum(gam[:, :], ps_x[:, 0:4].rearrange("p (m k) -> p m k", m=2), AX_X
                                     ).then_inc(thr_step, 1)
                dve.wait_ge(thr_step, 1)
                nc.vector.tensor_scalar(thr[:, :], gam[:, :], 1.0 / (D * F), GAMMA_EPS, ALU.mult, ALU.add
                                        ).then_inc(thr_step, 1)
                dve.wait_ge(thr_step, 2)
                nc.vector.tensor_scalar(nthr[:, :], thr[:, :], -0.5, None, ALU.mult).then_inc(thr_step, 1)
                dve.wait_ge(thr_step, 3)
                nc.vector.tensor_scalar(thr[:, :], nthr[:, :], -1.0, None, ALU.mult).then_inc(thr_step, 1)
                dve.wait_ge(thr_step, 4)
                for k in range(4):
                    m = k // 2
                    raw = fraw[:, m, k % 2 * F:(k % 2 + 1) * F]
                    dst = wfc[:, k, :] if m == 0 else wpj[:, 4 * (k - 2):4 * (k - 1), :].rearrange("p j n -> p (j n)")
                    if k:
                        dve.wait_ge(tern_ready, k)
                    nc.vector.tensor_scalar(stage[:, :], raw, nthr[:, m:m + 1], None, ALU.is_lt).then_inc(tern_neg, 1)
                    dve.wait_ge(tern_neg, k + 1)
                    nc.vector.scalar_tensor_tensor(out=dst, in0=raw, scalar=thr[:, m:m + 1], in1=stage[:, :],
                                                   op0=ALU.is_gt, op1=ALU.subtract).then_inc(tern_ready, 1)

            def b_step(i, n):
                if n is not None:
                    x_stats(X, n)
                max_sub(X, i, 0)
                if n is not None:
                    x_norm(X, n)
                max_sub(X, i, 1)
                row_sum(X, i, 0)
                if n is not None:
                    x_lo(X, n)
                for t in range(1, 4):
                    max_sub(X, i, t + 1)
                    row_sum(X, i, t)
                for t in range(4, 7):
                    max_sub(X, i, t + 1)
                    o_lo(X, i, t - 4)
                    row_sum(X, i, t)
                o_lo(X, i, 3)
                row_sum(X, i, 7)
                if n is None:
                    ternarise()
                for t in range(4, 7):
                    o_lo(X, i, t)
                o_lo(X, i, 7)
                if n is not None:
                    b_k(n, 2, 8)
                    b_k(n, 3, 9)
                resid(X, i, ps_x)
            b_step(0, 1)
            with dve.Fori(1, G - 1) as i:
                b_step(i, i + 1)
            b_step(G - 1, None)

            def g_stats(n, b):
                dve.wait_ge(C.g_ready, 2 * (NB * n + b + 1))
                for s in range(2):
                    last = nc.vector.bn_stats(gstats[:, b, s, :], g[:, b, s * 512:(s + 1) * 512])
                last.then_inc(C.gstats_done, 1)
                dve.wait_ge(C.gstats_done, NB * n + b + 1)
                nc.vector.memset(scratch[:, :], 0.0)
                nc.vector.bn_aggr(gmv[:, b, :], gstats[:, b, :, :].rearrange("p s k -> p (s k)")).then_inc(C.gaggr_done, 1)
                dve.wait_ge(C.gaggr_done, NB * n + b + 1)
                nc.vector.tensor_scalar(gvareps[:, b:b + 1], gmv[:, b, 1:2], LN_EPS, None, ALU.add
                                        ).then_inc(C.gvareps_done, 1)

            def g_norm(n, b):
                nc.vector.scalar_tensor_tensor(out=g[:, b, :], in0=g[:, b, :], scalar=gmv[:, b, 0:1],
                                               in1=lnw_bc[:, :], op0=ALU.subtract, op1=ALU.mult).then_inc(C.gscaled, 1)
                dve.wait_ge(C.gscaled, NB * n + b + 1)
                dve.wait_ge(C.grstd_ready, NB * n + b + 1)
                nc.vector.scalar_tensor_tensor(out=g[:, b, :], in0=g[:, b, :], scalar=grstd[:, b:b + 1],
                                               in1=lnb_bc[:, :], op0=ALU.mult, op1=ALU.add).then_inc(C.gn_ready, 1)

            def h_lo(i, b):
                for s in range(2):
                    dve.wait_ge(C.hh_ready, 2 * (NB * i + b) + s + 1)
                    tt(hTl[:, b, 4 * s:4 * s + 4, :], ps_s[s][:, :].rearrange("p (j n) -> p j n", j=4),
                       f32(hTh[:, b, 4 * s:4 * s + 4, :]), ALU.subtract).then_inc(C.hl_ready, 1)

            dve.wait_ge(X.resid_done, G)
            dve.wait_ge(ld_ln, 32)
            x_stats(C, 0)
            x_norm(C, 0)
            x_lo(C, 0)
            for b in range(NB):
                g_stats(0, b)
                g_norm(0, b)

            def c_step(i, n):
                if n is not None:
                    x_stats(C, n)
                    x_norm(C, n)
                h_lo(i, 0)
                if n is not None:
                    x_lo(C, n)
                    g_stats(n, 0)
                h_lo(i, 1)
                if n is not None:
                    g_norm(n, 0)
                    g_stats(n, 1)
                resid(C, i, ps_o[0])
                if n is not None:
                    g_norm(n, 1)
            c_step(0, 1)
            with dve.Fori(1, G - 1) as i:
                c_step(i, i + 1)
            c_step(G - 1, None)

        @block.gpsimd
        def _(pool):
            tt = nc.gpsimd.tensor_tensor

            def x_rstd(ph, n):
                pool.wait_ge(ph.vareps_done, n + 1)
                tt(rstd[:, :], vareps[:, :], neghalf[:, :], ALU.pow).then_inc(ph.rstd_ready, 1)

            def p_norm(ph, i, t):
                pool.wait_ge(ph.rc_ready, i * ph.T + t + 1)
                p = prob[:, t % 4, :].rearrange("p (h k) -> p h k", h=TH)
                tt(p, p, bcast(rc[:, t % 4, :], P), ALU.mult).then_inc(ph.normed, 1)

            def a_rotate(n, c):
                pool.wait_ge(A.roped, 4 * n + c + 1)
                if not (isinstance(n, int) and n == 0):
                    wait_if(pool, A.s_ready, n * T1)
                mc, ms = ropec[:, c % 2, :, :], ropes[:, c % 2, :, :]
                for ab, op in ((0, ALU.subtract), (1, ALU.add)):
                    if c < 2:
                        last = tt(qA[:, c, ab, :], mc[:, ab, :], ms[:, 1 - ab, :], op)
                    else:
                        for h in range(TH):
                            m = TH * ab + h
                            if m:
                                wait_if(pool, A.k_step, 14 * n + 7 * (c - 2) + m)
                            else:
                                wait_if(pool, A.qk_ready, 4 * n + c)
                            r = slice(32 * h, 32 * h + 32)
                            last = tt(kA[r, c - 2, ab, :, h, :],
                                      ropec[r, c % 2, ab, :].rearrange("p (b n) -> p b n", b=NB),
                                      ropes[r, c % 2, 1 - ab, :].rearrange("p (b n) -> p b n", b=NB), op)
                            if m < 2 * TH - 1:
                                last.then_inc(A.k_step, 1)
                last.then_inc(A.qk_ready, 1)
                if c == 3:
                    pool.wait_ge(A.qk_ready, 4 * n + 4)

            def w2_split(i):
                pool.wait_ge(ld_w2, 16 * (i + 1))
                hi, lo = (w2[:, k, bass.ds(i, 1), :].rearrange("p a n -> p (a n)") for k in range(2))
                nc.gpsimd.tensor_copy(hi, stage[:, :]).then_inc(w2_hi, 1)
                pool.wait_ge(w2_hi, i + 1)
                tt(lo, stage[:, :], f32(hi), ALU.subtract).then_inc(w2_ready, 1)

            nc.gpsimd.memset(neghalf[:, :], -0.5)
            nc.gpsimd.memset(kA[:, :, :, :, :, :], 0.0).then_inc(k_zeroed, 1)
            nc.gpsimd.memset(ones_t[:, :], 1.0).then_inc(ones_ready, 1)
            pool.wait_ge(ones_ready, 1)
            pool.wait_ge(k_zeroed, 1)
            x_rstd(A, 0)
            pool.wait_ge(ld_wo, 16)
            nc.gpsimd.tensor_copy(woh[:, :, :], woraw[:, :, :]).then_inc(woh_done, 1)
            pool.wait_ge(woh_done, 1)
            tt(wol[:, :, :], woraw[:, :, :], f32(woh[:, :, :]), ALU.subtract).then_inc(wo_ready, 1)
            for c in range(4):
                a_rotate(0, c)
            pool.wait_ge(w1l_ready, 1)
            pool.wait_ge(wo_ready, 1)

            def a_step(i, n):
                if n is not None:
                    x_rstd(A, n)
                p_norm(A, i, 0)
                p_norm(A, i, 1)
                p_norm(A, i, 2)
                if n is not None:
                    a_rotate(n, 0)
                p_norm(A, i, 3)
                if n is not None:
                    a_rotate(n, 1)
                    a_rotate(n, 2)
                    a_rotate(n, 3)
                w2_split(i)
            a_step(0, 1)
            with pool.Fori(1, G - 1) as i:
                a_step(i, i + 1)
            a_step(G - 1, None)

            def ctx_split(n):
                wait_if(pool, X.pj_ready, n * X.U)
                pool.wait_ge(X.ch_done, n + 1)
                tt(cl[:, :, :], craw[:, :, :], f32(ch[:, :, :]), ALU.subtract).then_inc(X.cl_ready, 1)

            x_rstd(X, 0)
            pool.wait_ge(w2_ready, WP)
            pool.wait_ge(X.rstd_ready, 1)
            pool.wait_ge(A.s_ready, T1 * G)
            nc.gpsimd.memset(kB[HD:P, :, :, 0, :].rearrange("p j b n -> p (j b) n"), 0.0).then_inc(kB_zeroed, 1)
            pool.wait_ge(kB_zeroed, 2)
            ctx_split(0)

            def b_step(i, n):
                if n is not None:
                    x_rstd(X, n)
                for t in range(T2):
                    p_norm(X, i, t)
                    if n is not None and t == 1:
                        ctx_split(n)
            b_step(0, 1)
            with pool.Fori(1, G - 1) as i:
                b_step(i, i + 1)
            b_step(G - 1, None)

            def g_rstd(n, b):
                pool.wait_ge(C.gvareps_done, NB * n + b + 1)
                tt(grstd[:, b:b + 1], gvareps[:, b:b + 1], neghalf[:, 0:1], ALU.pow).then_inc(C.grstd_ready, 1)

            x_rstd(C, 0)
            g_rstd(0, 0)
            g_rstd(0, 1)
            with pool.Fori(1, G) as n:
                x_rstd(C, n)
                g_rstd(n, 0)
                g_rstd(n, 1)


def _constants():
    import numpy as np
    inv = (1.0 / np.float32(10000.0) ** (np.arange(0, HD, 2, dtype=np.float32) / np.float32(HD))).astype(np.float32)
    ang = (np.arange(T, dtype=np.float32)[None, :] * inv[:, None]).astype(np.float32)
    cos, sin = np.tile(np.cos(ang), (TH, 1)), np.tile(np.sin(ang), (TH, 1))
    q, k = np.arange(T)[:, None], np.arange(T)[None, :]
    window = np.where((k <= q) & (k > q - 64), 0.0, -1e30)
    causal = np.where(k <= q, 0.0, -1e30)
    return np.concatenate([cos, sin, np.eye(P), window, causal], axis=1).astype(np.float32)


def kernel(x, ctx_1024, L0_attn_Wqkv, L0_attn_Wout, L0_xattn_w_q, L0_xattn_w_k, L0_xattn_w_v, L0_xattn_w_o,
           L0_ffn_W_fc, L0_ffn_ln_w, L0_ffn_ln_b, L0_ffn_W_proj):
    import numpy as np
    import concourse.bacc as bacc
    from concourse.bass_utils import run_bass_kernel_spmd

    wqkv = np.asarray(L0_attn_Wqkv)
    qk = wqkv[:, :2 * I1].reshape(D, 2, 2, TH, 2, 32).transpose(0, 1, 2, 4, 3, 5).reshape(D, 2 * I1)
    wqkv = np.concatenate([qk, wqkv[:, 2 * I1:]], axis=1)
    proj = [np.asarray(w).T.reshape(DC, P, I2) for w in (L0_xattn_w_q, L0_xattn_w_k, L0_xattn_w_v)]
    wo = np.asarray(L0_xattn_w_o).T.reshape(2, 4, P, D).transpose(0, 2, 1, 3).reshape(2, P, 4 * D)
    arrays = {
        "x": np.asarray(x).reshape(B * T, D),
        "ctxT": np.asarray(ctx_1024).reshape(B * T, D).T,
        "wqkv": wqkv,
        "wout": np.asarray(L0_attn_Wout),
        "wx": np.concatenate(proj + [wo], axis=0),
        "wfcT": np.asarray(L0_ffn_W_fc).T,
        "wprojT": np.asarray(L0_ffn_W_proj).T,
        "lnw": np.asarray(L0_ffn_ln_w),
        "lnb": np.asarray(L0_ffn_ln_b),
        "tables": _constants(),
    }
    arrays = {k: np.ascontiguousarray(v) for k, v in arrays.items()}
    nc = bacc.Bacc("TRN2", target_bir_lowering=False, num_devices=1)
    aps = [nc.dram_tensor(k, v.shape, mybir.dt.from_np(v.dtype), kind="ExternalInput").ap() for k, v in arrays.items()]
    out = nc.dram_tensor("out", (B * T, D), F32, kind="ExternalOutput").ap()
    decoder_program(nc, *aps, out)
    r = run_bass_kernel_spmd(nc, [arrays], core_ids=[0])
    return r.results[0]["out"].reshape(B, T, D)
```

```python
from contextlib import ExitStack

import concourse.bass as bass
from concourse import mybir

F32 = mybir.dt.float32
F32R = mybir.dt.float32r
BF16 = mybir.dt.bfloat16
ALU = mybir.AluOpType
ACT = mybir.ActivationFunctionType
AX_X = mybir.AxisListType.X

P = 128
B, T, D = 16, 128, 256
NB = 2
G = B // NB
GT = NB * T
DC = D // P
HD = 64
H1 = 8
H2 = 16
I1 = H1 * HD
I2 = H2 * HD
F = 1024
FC = F // P
TH = 4
T1 = NB * H1 // TH
T2 = NB * H2 // TH
WP = 8
SCALE = HD ** -0.5
LN_EPS = 1e-5
GAMMA_EPS = 1e-6


class Norm:

    def __init__(self, sb, tag, xn, xh, xl):
        self.xn = xn
        self.xh = xh
        self.xl = xl
        self.stats = sb(tag + "_stats", [P, NB, 6])
        self.mv = sb(tag + "_mv", [P, NB, 2])
        self.vareps = sb(tag + "_vareps", [P, NB])
        self.rstd = sb(tag + "_rstd", [P, NB])


class Phase:

    def __init__(self, sem, norm, tag, units, tiles=0):
        self.norm = norm
        self.U = units
        self.T = tiles
        self.stats_done = sem(tag + "_stats_done")
        self.aggr_done = sem(tag + "_aggr_done")
        self.vareps_done = sem(tag + "_vareps_done")
        self.rstd_ready = sem(tag + "_rstd_ready")
        self.xn_ready = sem(tag + "_xn_ready")
        self.lnt_done = sem(tag + "_lnt_done")
        self.xh_ready = sem(tag + "_xh_ready")
        self.xl_ready = sem(tag + "_xl_ready")
        self.pj_ready = sem(tag + "_pj_ready")
        self.out_ready = sem(tag + "_out_ready")
        self.resid_done = sem(tag + "_resid_done")


class AttentionPhase(Phase):
    def __init__(self, sem, norm, tag, units, tiles):
        super().__init__(sem, norm, tag, units, tiles)
        self.s_ready = sem(tag + "_s_ready")
        self.maxed = sem(tag + "_maxed")
        self.subbed = sem(tag + "_subbed")
        self.exped = sem(tag + "_exped")
        self.summed = sem(tag + "_summed")
        self.rc_ready = sem(tag + "_rc_ready")
        self.normed = sem(tag + "_normed")
        self.transposed = sem(tag + "_transposed")
        self.pt_ready = sem(tag + "_pt_ready")
        self.av_done = sem(tag + "_av_done")
        self.oh_ready = sem(tag + "_oh_ready")
        self.ol_ready = sem(tag + "_ol_ready")
        self.v_ready = sem(tag + "_v_ready")

    def tile(self, t):
        raise NotImplementedError

    def tiles_of(self, b):
        return max(t for t in range(self.T) if self.tile(t)[0] == b) + 1


class SelfPhase(AttentionPhase):
    def __init__(self, sem, norm, tag, units, tiles):
        super().__init__(sem, norm, tag, units, tiles)
        self.roped = sem(tag + "_roped")
        self.rotated = sem(tag + "_rotated")
        self.qk_ready = sem(tag + "_qk_ready")

    def tile(self, t):
        return t % NB, t // NB


class CrossPhase(AttentionPhase):
    def __init__(self, sem, norm, tag, units, tiles):
        super().__init__(sem, norm, tag, units, tiles)
        self.ch_done = sem(tag + "_ch_done")
        self.cl_ready = sem(tag + "_cl_ready")
        self.q_ready = sem(tag + "_q_ready")
        self.ka_ready = sem(tag + "_ka_ready")
        self.kd_ready = sem(tag + "_kd_ready")

    def tile(self, t):
        return t // TH, t % TH


class FfnPhase(Phase):
    def __init__(self, sem, norm, tag, units):
        super().__init__(sem, norm, tag, units)
        self.g_ready = sem(tag + "_g_ready")
        self.gstats_done = sem(tag + "_gstats_done")
        self.gaggr_done = sem(tag + "_gaggr_done")
        self.gvareps_done = sem(tag + "_gvareps_done")
        self.grstd_ready = sem(tag + "_grstd_ready")
        self.gscaled = sem(tag + "_gscaled")
        self.cb_added = sem(tag + "_cb_added")
        self.gn_ready = sem(tag + "_gn_ready")
        self.gt_ready = sem(tag + "_gt_ready")
        self.hh_ready = sem(tag + "_hh_ready")
        self.hl_ready = sem(tag + "_hl_ready")


def decoder_program(nc, x_d, ctxT_d, wqkv_d, wout_d, wx_d, wfcT_d, wprojT_d, lnw_d, lnb_d, const_d, out_d):
    with ExitStack() as ctx:
        nxt = [nc.sbuf_base + (-nc.sbuf_base) % 32]

        def region(nbytes):
            at = nxt[0]
            nxt[0] = at + nbytes
            return at

        def sb(name, shape, dt=F32, at=None):
            n = 2 if dt == BF16 else 4
            for s in shape[1:]:
                n *= s
            if at is None:
                at = region(n + (-n) % 32)
            return nc.alloc_sbuf_tensor_at(name, shape, dt, offset=at)

        def sem(name):
            return ctx.enter_context(nc.semaphore(name))

        x_sb = sb("x_sb", [P, B, D])
        r_const = region(3 * P * 4)
        const = sb("const", [P, 3, P], at=r_const)
        cos_t, sin_t, ident = const[:, 0, :], const[:, 1, :], const[:, 2, :]
        mask_w = sb("mask_w", [P, TH, P], BF16)
        mask_c = sb("mask_c", [P, TH, P], BF16)
        ident_b = sb("ident_b", [P, P], BF16)
        ones_t = sb("ones_t", [P, P])
        lnw_bc = sb("lnw_bc", [P, F])
        lnb_col = sb("lnb_col", [P, FC])
        cb = sb("cb", [P, D], at=r_const)
        scratch = sb("scratch", [P, 1])
        neghalf = sb("neghalf", [P, NB])
        norm_x = Norm(sb, "x", sb("xn", [P, NB, D]), sb("xh", [P, DC, GT], F32R), sb("xl", [P, DC, GT], F32R))
        mx = sb("mx", [P, 4, TH])
        sm = sb("sm", [P, 4, TH])
        rc = sb("rc", [P, 4, TH])
        r_prob = region(4 * TH * P * 4)
        mask_raw = sb("mask_raw", [P, 2, P], at=r_prob)
        prob = sb("prob", [P, 4, TH * P], at=r_prob)
        probT = sb("probT", [P, 2, TH * P])
        oh = sb("oh", [P, NB, H2 // 2, P], F32R)
        ol = sb("ol", [P, NB, H2 // 2, P], F32R)
        r_stage = region(4096)
        stage = sb("stage", [P, F], at=r_stage)
        r_g = region(F * 4)
        ropes = sb("ropes", [P, 2, 2, GT], at=r_g)
        g = [sb("g0", [P, F], at=r_g), sb("g1", [P, F])]
        gstats = sb("gstats", [P, NB, 2, 6])
        gmv = sb("gmv", [P, NB, 2])
        gvareps = sb("gvareps", [P, NB])
        grstd = sb("grstd", [P, NB])
        asum = sb("asum", [P, 4])
        gam = sb("gam", [P, 2])
        thr = sb("thr", [P, 2])
        nthr = sb("nthr", [P, 2])

        r_q = region(H2 // 2 * GT * 4)
        q_t = sb("q_t", [P, H2 // 2, GT], at=r_q)
        r_k = region(16384)
        k_t = sb("k_t", [P, H2 // 2, NB, 2, P], at=r_k)
        r_v = region(8192)
        vA = sb("vA", [P, NB, I1], at=r_v + 4096)
        vB = sb("vB", [P, NB, I2], at=r_v)
        r_m = region(8192)
        ropec = sb("ropec", [P, 4, 2, GT], at=r_m)
        craw = sb("craw", [P, DC, GT], at=r_m)
        ch = sb("ch", [P, DC, GT], F32R, at=r_m + 2048)
        cl = sb("cl", [P, DC, GT], F32R, at=r_m + 4096)
        norm_f = Norm(sb, "f", sb("fn", [P, NB, D], at=r_m + 6144), sb("fh", [P, DC, GT], F32R, at=r_stage),
                      sb("fl", [P, DC, GT], F32R, at=r_stage + 2048))
        r_1 = region(32768)
        w1h = sb("w1h", [P, DC, 3 * I1], F32R, at=r_1)
        w1l = sb("w1l", [P, DC, 3 * I1], F32R, at=r_1 + 12288)
        woh = sb("woh", [P, I1 // P, D], F32R, at=r_1 + 24576)
        wol = sb("wol", [P, I1 // P, D], F32R, at=r_1 + 28672)
        fraw = sb("fraw", [P, 2, DC * F], at=r_1)
        hTh = sb("hTh", [P, NB, FC, P], F32R, at=r_1)
        hTl = sb("hTl", [P, NB, FC, P], F32R, at=r_1 + 8192)
        bh = sb("bh", [P, FC, P], F32R, at=r_1)
        bl = sb("bl", [P, FC, P], F32R, at=r_1 + 4096)
        wfc = sb("wfc", [P, DC, F], F32R, at=r_1 + 16384)
        wpj = sb("wpj", [P, FC, D], F32R, at=r_1 + 24576)
        r_2 = region(65536)
        w1raw = sb("w1raw", [P, DC, 3 * I1], at=r_2)
        woraw = sb("woraw", [P, I1 // P, D], at=r_2 + 12288)
        w2 = sb("w2", [P, 2, WP, F], F32R, at=r_2)
        assert nxt[0] <= nc.sbuf_usable_end, nxt[0]

        def ps(name):
            return ctx.enter_context(nc.psum_tensor(name, [P, 512], F32))
        ps_s = [ps("ps_s0"), ps("ps_s1")]
        ps_t = ps("ps_t")
        ps_p = [ps("ps_p0"), ps("ps_p1")]
        ps_o = [ps("ps_o0"), ps("ps_o1")]
        ps_x = ps("ps_x")

        ld_x0, ld_xr, ld_c, ld_m, ld_wo, ld_ln = (sem(n) for n in ("ld_x0", "ld_xr", "ld_c", "ld_m", "ld_wo", "ld_ln"))
        ld_w1a, ld_w1b, ld_w1c = (sem(n) for n in ("ld_w1a", "ld_w1b", "ld_w1c"))
        ld_w2, ld_ctx, ld_f, st_out = (sem(n) for n in ("ld_w2", "ld_ctx", "ld_f", "st_out"))
        masks_ready, k_zeroed, ones_ready = (sem(n) for n in ("masks_ready", "k_zeroed", "ones_ready"))
        w1h_ready, w1l_ready, wo_ready, woh_done = (sem(n) for n in ("w1h_ready", "w1l_ready", "wo_ready", "woh_done"))
        bh_ready, bl_ready, cb_summed, cb_ready = (sem(n) for n in ("bh_ready", "bl_ready", "cb_summed", "cb_ready"))
        w2_hi, w2_ready = sem("w2_hi"), sem("w2_ready")
        abs_summed, gam_summed, thr_step, tern_neg, tern_ready = (
            sem(n) for n in ("abs_summed", "gam_summed", "thr_step", "tern_neg", "tern_ready"))

        A = SelfPhase(sem, norm_x, "a", 6, T1)
        X = CrossPhase(sem, norm_x, "b", 12, T2)
        C = FfnPhase(sem, norm_f, "c", 4)

        def bcast(ap, n):
            return ap.unsqueeze(2).to_broadcast([P, ap.shape[1], n])

        def f32(ap):
            return ap.bitcast(F32)

        def wait_if(engine, semaphore, value):
            if not isinstance(value, int) or value > 0:
                engine.wait_ge(semaphore, value)

        block = ctx.enter_context(nc.Block())

        @block.sync
        def _(sp):
            x_v = x_d.rearrange("(b t) d -> t b d", t=T)
            sp.dma_start(x_sb[:, 0:NB, :], x_v[:, 0:NB, :]).then_inc(ld_x0, 16)
            sp.dma_start(const[:, :, :], const_d[:, 0:3 * P].rearrange("p (k n) -> p k n", k=3)).then_inc(ld_c, 16)
            w1_v = wqkv_d.rearrange("(c p) n -> p c n", p=P)
            for ld, k in ((ld_w1a, 0), (ld_w1b, 1), (ld_w1c, 2)):
                sp.dma_start(w1raw[:, :, k * I1:(k + 1) * I1], w1_v[:, :, k * I1:(k + 1) * I1]).then_inc(ld, 16)
            sp.dma_start(mask_raw[:, :, :], const_d[:, 3 * P:].rearrange("p (k n) -> p k n", k=2)).then_inc(ld_m, 16)
            sp.dma_start(woraw[:, :, :], wout_d.rearrange("(c p) n -> p c n", p=P)).then_inc(ld_wo, 16)
            sp.dma_start(x_sb[:, NB:B, :], x_v[:, NB:B, :]).then_inc(ld_xr, 16)
            sp.dma_start(lnw_bc[:, :], lnw_d.partition_broadcast(P)).then_inc(ld_ln, 16)
            sp.dma_start(lnb_col[:, :], lnb_d).then_inc(ld_ln, 16)

            def w2_load(i):
                wait_if(sp, w2_ready, i)
                sp.dma_start(stage[:, :], wx_d[bass.ds(i, 1), :, :].rearrange("a p n -> p (a n)")).then_inc(ld_w2, 16)
            w2_load(0)
            with sp.Fori(1, WP) as i:
                w2_load(i)

            ctx_v = ctxT_d.rearrange("(c p) n -> p c n", p=P)

            def ctx_load(n):
                wait_if(sp, X.cl_ready, n)
                sp.dma_start(craw[:, :, :], ctx_v[:, :, bass.ds(n * GT, GT)]).then_inc(ld_ctx, 16)
            sp.wait_ge(A.qk_ready, 4 * G)
            ctx_load(0)
            sp.wait_ge(A.out_ready, NB * G)
            sp.dma_start(fraw[:, 0, :].rearrange("p (c n) -> p c n", c=DC),
                         wfcT_d.rearrange("(c p) n -> p c n", p=P)).then_inc(ld_f, 16)
            sp.dma_start(fraw[:, 1, :].rearrange("p (c n) -> p c n", c=FC),
                         wprojT_d.rearrange("(c p) n -> p c n", p=P)).then_inc(ld_f, 16)
            with sp.Fori(1, G) as n:
                ctx_load(n)

            out_v = out_d.rearrange("(b t) d -> t b d", t=T)
            with sp.Fori(0, G) as i:
                sp.wait_ge(C.resid_done, i + 1)
                sp.dma_start(out_v[:, bass.ds(NB * i, NB), :], x_sb[:, bass.ds(NB * i, NB), :]).then_inc(st_out, 16)
            sp.wait_ge(st_out, 16 * G)

        @block.tensor
        def _(pe):
            mm = nc.tensor.matmul
            xh, xl, fh, fl = norm_x.xh, norm_x.xl, norm_f.xh, norm_f.xl

            def product(out, lh, ll, rh, rl, first, last):
                mm(out, lh, rh, start=first, stop=False)
                mm(out, lh, rl, start=False, stop=False)
                return mm(out, ll, rh, start=False, stop=last)

            def ln_transposes(ph, n):
                pe.wait_ge(ph.xn_ready, n + 1)
                for b in range(NB):
                    for c in range(DC):
                        last = nc.tensor.transpose(ps_x[:, c * GT + b * T:c * GT + (b + 1) * T],
                                                   ph.norm.xn[:, b, c * P:(c + 1) * P], ident)
                last.then_inc(ph.lnt_done, 1)

            def unit_bank(freed, n, u, between=None):
                done, per_group, count = freed[u]
                wait_if(pe, done, n * per_group + count)
                if between is not None:
                    pe.wait_ge(between[0], between[1] + u % 2)
                return ps_p[u % 2]

            a_freed = [(A.v_ready, 2, 0), (A.v_ready, 2, 0), (A.roped, 4, 1), (A.roped, 4, 2), (A.roped, 4, 3),
                       (A.roped, 4, 4)]
            x_freed = [(X.v_ready, 4, 0), (X.v_ready, 4, 0), (X.v_ready, 4, 1), (X.v_ready, 4, 2),
                       (X.q_ready, 4, 1), (X.q_ready, 4, 2), (X.q_ready, 4, 3), (X.q_ready, 4, 4),
                       (X.ka_ready, 2, 1), (X.ka_ready, 2, 2), (X.kd_ready, 2, 1), (X.kd_ready, 2, 2)]

            def scores(ph, i, t, mask):
                b, q = ph.tile(t)
                wait_if(pe, ph.subbed, i * ph.T + max(t - 1, 0))
                mm(ps_s[t % 2][:, :], ident_b[:, :], mask[:, :, :], start=True, stop=False)
                for s in range(2):
                    pair = 2 * q + s
                    last = mm(ps_s[t % 2][:, s * 2 * P:(s + 1) * 2 * P], q_t[:, pair, b * T:(b + 1) * T],
                              k_t[:, pair, b, :, :], start=False, stop=s == 1)
                last.then_inc(ph.s_ready, 1)

            def tr(ph, i, t):
                pe.wait_ge(ph.normed, i * ph.T + t + 1)
                wait_if(pe, ph.pt_ready, i * ph.T + t)
                for h in range(TH):
                    last = nc.tensor.transpose(ps_t[:, h * P:(h + 1) * P],
                                               prob[:, t % 4, h * P:(h + 1) * P], ident)
                last.then_inc(ph.transposed, 1)

            def av(ph, i, t, v):
                pe.wait_ge(ph.pt_ready, i * ph.T + t + 1)
                wait_if(pe, ph.ol_ready, i * ph.T + max(t - 1, 0))
                b, q = ph.tile(t)
                for h in range(TH):
                    head, col = q * TH + h, (h // 2) * P
                    last = mm(ps_o[t % 2][HD * (h % 2):HD * (h % 2 + 1), col:col + P],
                              v[:, b, head * HD:(head + 1) * HD], probT[:, t % 2, h * P:(h + 1) * P],
                              start=True, stop=True)
                last.then_inc(ph.av_done, 1)

            def project_out(ph, i, b, wh, wl, nj):
                pe.wait_ge(ph.ol_ready, i * ph.T + ph.tiles_of(b))
                for j in range(nj):
                    last = product(ps_x[:, b * D:(b + 1) * D], oh[:, b, j, :], ol[:, b, j, :], wh(j), wl(j),
                                   j == 0, j == nj - 1)
                last.then_inc(ph.out_ready, 1)

            def a_qk(n, c):
                bank = unit_bank(a_freed, n, c)
                pe.wait_ge(A.xl_ready, n + 1)
                for ab in range(2):
                    col = (2 * c + ab) * P
                    for d in range(DC):
                        last = product(bank[:, ab * GT:(ab + 1) * GT], w1h[:, d, col:col + P], w1l[:, d, col:col + P],
                                       xh[:, d, :], xl[:, d, :], d == 0, d == DC - 1)
                last.then_inc(A.pj_ready, 1)

            def a_v(n, b):
                bank = unit_bank(a_freed, n, 4 + b)
                for d in range(DC):
                    last = product(bank[:, :], xh[:, d, b * T:(b + 1) * T], xl[:, d, b * T:(b + 1) * T],
                                   w1h[:, d, 2 * I1:], w1l[:, d, 2 * I1:], d == 0, d == DC - 1)
                last.then_inc(A.pj_ready, 1)

            def a_s(i, t):
                pe.wait_ge(A.qk_ready, 4 * i + 2 * (t // NB) + 2)
                scores(A, i, t, mask_w)

            def a_out(i, b):
                project_out(A, i, b, lambda j: woh[:, j, :], lambda j: wol[:, j, :], I1 // P)

            def wx(k, piece, lo, hi):
                return w2[:, k, piece, lo:hi]

            def b_pairs(n, c, u, base, src_h, src_l, ready, between):
                bank = unit_bank(x_freed, n, u, between)
                pe.wait_ge(ready, n + 1)
                for s in range(2):
                    col = (2 * c + s) * P
                    for d in range(DC):
                        last = product(bank[:, s * GT:(s + 1) * GT], wx(0, base + d, col, col + P),
                                       wx(1, base + d, col, col + P), src_h[:, d, :], src_l[:, d, :],
                                       d == 0, d == DC - 1)
                last.then_inc(X.pj_ready, 1)

            def b_q(n, c, between=None):
                b_pairs(n, c, 2 + c, 0, xh, xl, X.xl_ready, between)

            def b_k(n, c, between=None):
                b_pairs(n, c, 6 + c, 2, ch, cl, X.cl_ready, between)

            def b_v(n, b, s, between=None):
                bank = unit_bank(x_freed, n, 10 * b + s, between)
                pe.wait_ge(X.cl_ready, n + 1)
                for d in range(DC):
                    last = product(bank[:, :], ch[:, d, b * T:(b + 1) * T], cl[:, d, b * T:(b + 1) * T],
                                   wx(0, 4 + d, s * 512, s * 512 + 512), wx(1, 4 + d, s * 512, s * 512 + 512),
                                   d == 0, d == DC - 1)
                last.then_inc(X.pj_ready, 1)

            def b_s(i, t):
                pe.wait_ge(X.q_ready, 4 * i + 4)
                pe.wait_ge(X.ka_ready, 2 * i + 2)
                pe.wait_ge(X.kd_ready, 2 * i + 2)
                scores(X, i, t, mask_c)

            def b_out(i, b):
                project_out(X, i, b, lambda j: wx(0, 6 + j // 4, j % 4 * D, j % 4 * D + D),
                            lambda j: wx(1, 6 + j // 4, j % 4 * D, j % 4 * D + D), I2 // P)

            def c_fc(m, b, freed, count):
                pe.wait_ge(C.xl_ready, m + 1)
                for s in range(2):
                    wait_if(pe, freed, count + s)
                    for d in range(DC):
                        w = wfc[:, d, s * 512:(s + 1) * 512]
                        mm(ps_p[s][:, :], fh[:, d, b * T:(b + 1) * T], w, start=d == 0, stop=False)
                        last = mm(ps_p[s][:, :], fl[:, d, b * T:(b + 1) * T], w, start=False, stop=d == DC - 1)
                    last.then_inc(C.pj_ready, 1)

            def c_tr(m, b, freed, count):
                pe.wait_ge(C.gn_ready, NB * m + b + 1)
                for s in range(2):
                    pe.wait_ge(freed, count + s)
                    for j in range(4):
                        last = nc.tensor.transpose(ps_p[s][:, j * P:(j + 1) * P],
                                                   g[b][:, (4 * s + j) * P:(4 * s + j + 1) * P], ident)
                    last.then_inc(C.gt_ready, 1)

            def c_out(m, b, bank):
                pe.wait_ge(C.hl_ready, 2 * (NB * m + b + 1))
                for j in range(FC):
                    mm(bank[:, b * D:(b + 1) * D], hTh[:, b, j, :], wpj[:, j, :], start=j == 0, stop=False)
                    last = mm(bank[:, b * D:(b + 1) * D], hTl[:, b, j, :], wpj[:, j, :],
                              start=False, stop=j == FC - 1)
                last.then_inc(C.out_ready, 1)

            pe.wait_ge(ld_c, 16)
            ln_transposes(A, 0)
            for c in range(4):
                pe.wait_ge(w1l_ready, c // 2 + 1)
                a_qk(0, c)
            pe.wait_ge(w1l_ready, 3)
            a_v(0, 0)
            pe.wait_ge(masks_ready, 3)
            pe.wait_ge(k_zeroed, 1)

            def a_start(i, ph, n):
                a_s(i, 0)
                a_s(i, 1)
                if not (isinstance(i, int) and i == 0):
                    a_out(i - 1, 0)
                    a_out(i - 1, 1)
                a_s(i, 2)
                a_v(i, 1)
                tr(A, i, 0)
                wait_if(pe, A.resid_done, i)
                ln_transposes(ph, n)
                a_s(i, 3)
                pe.wait_ge(A.v_ready, NB * i + NB)
                av(A, i, 0, vA)
                tr(A, i, 1)

            def a_step(i):
                n = i + 1
                a_start(i, A, n)
                a_qk(n, 0)
                av(A, i, 1, vA)
                a_qk(n, 1)
                tr(A, i, 2)
                a_qk(n, 2)
                av(A, i, 2, vA)
                a_qk(n, 3)
                tr(A, i, 3)
                a_v(n, 0)
                av(A, i, 3, vA)
            a_step(0)
            pe.wait_ge(wo_ready, 1)
            with pe.Fori(1, G - 1) as i:
                a_step(i)
            i = G - 1
            a_start(i, X, 0)
            pe.wait_ge(w2_ready, WP - 1)
            pe.wait_ge(A.roped, 4 * G)
            b_v(0, 0, 0)
            av(A, i, 1, vA)
            b_v(0, 0, 1)
            tr(A, i, 2)
            b_q(0, 0)
            b_q(0, 1)
            av(A, i, 2, vA)
            tr(A, i, 3)
            b_q(0, 2)
            b_q(0, 3)
            av(A, i, 3, vA)
            for c in range(4):
                b_k(0, c)
            a_out(i, 0)
            a_out(i, 1)
            pe.wait_ge(w2_ready, WP)
            pe.wait_ge(k_zeroed, 3)

            def gamma_total():
                pe.wait_ge(abs_summed, 4)
                pe.wait_ge(ones_ready, 1)
                mm(ps_x[:, 0:4], ones_t[:, :], asum[:, :], start=True, stop=True).then_inc(gam_summed, 1)

            def bias_row():
                pe.wait_ge(bl_ready, 1)
                pe.wait_ge(X.kd_ready, 2 * 2 + 1)
                for j in range(FC):
                    mm(ps_p[0][:, 0:D], bh[:, j, :], wpj[:, j, :], start=j == 0, stop=False)
                    last = mm(ps_p[0][:, 0:D], bl[:, j, :], wpj[:, j, :], start=False, stop=j == FC - 1)
                last.then_inc(cb_summed, 1)

            def b_step(i, n, m, mo):
                b_s(i, 0)
                b_s(i, 1)
                if m is None:
                    pe.wait_ge(A.resid_done, G)
                else:
                    b_out(i - 1, 1)
                b_s(i, 2)
                if isinstance(i, int) and i == 2:
                    pe.wait_ge(cb_ready, 1)
                b_v(i, 1, 0)
                b_v(i, 1, 1)
                b_s(i, 3)
                if n is not None:
                    wait_if(pe, X.resid_done, i)
                    ln_transposes(X, n)
                tr(X, i, 0)
                b_s(i, 4)
                if mo is not None:
                    c_tr(mo, 0, X.v_ready, 4 * i + 3)
                pe.wait_ge(X.v_ready, 4 * i + 4)
                av(X, i, 0, vB)
                tr(X, i, 1)
                b_s(i, 5)
                if m is not None:
                    if n is not None:
                        pe.wait_ge(X.xl_ready, n + 1)
                    else:
                        pe.wait_ge(X.resid_done, i)
                    ln_transposes(C, m)
                av(X, i, 1, vB)
                tr(X, i, 2)
                b_s(i, 6)
                if mo is not None:
                    c_tr(mo, 1, C.hl_ready, 4 * mo + 1)
                av(X, i, 2, vB)
                tr(X, i, 3)
                b_s(i, 7)
                if mo is not None:
                    pe.wait_ge(C.xl_ready, m + 1)
                    c_out(mo, 0, ps_x)
                av(X, i, 3, vB)
                tr(X, i, 4)
                if mo is not None:
                    c_out(mo, 1, ps_x)
                av(X, i, 4, vB)
                if m is None:
                    b_v(n, 0, 0)
                else:
                    if isinstance(m, int) and m == 0:
                        pe.wait_ge(tern_ready, 4)
                    if mo is not None:
                        c_fc(m, 0, C.hl_ready, 4 * mo + 3)
                    else:
                        c_fc(m, 0, X.v_ready, 4 * i + 3)
                tr(X, i, 5)
                if m is None:
                    b_v(n, 0, 1)
                    pe.wait_ge(X.xl_ready, n + 1)
                    gamma_total()
                else:
                    c_fc(m, 1, C.g_ready, 4 * m + 1)
                av(X, i, 5, vB)
                tr(X, i, 6)
                if n is not None and m is not None:
                    for s in range(2):
                        b_v(n, 0, s, (C.g_ready, 4 * m + 3))
                av(X, i, 6, vB)
                if n is not None:
                    b_q(n, 0)
                    b_q(n, 1)
                tr(X, i, 7)
                if n is not None:
                    b_q(n, 2)
                    b_q(n, 3)
                av(X, i, 7, vB)
                if n is not None:
                    for c in range(4):
                        b_k(n, c)
                if m is None:
                    pe.wait_ge(thr_step, 1)
                elif mo is None:
                    pe.wait_ge(C.xl_ready, m + 1)
                else:
                    pe.wait_ge(C.resid_done, mo + 1)
                b_out(i, 0)
            b_step(0, 1, None, None)
            b_step(1, 2, 0, None)
            bias_row()
            b_step(2, 3, 1, 0)
            with pe.Fori(3, G - 1) as i:
                b_step(i, i + 1, i - 1, i - 2)
            b_step(G - 1, None, G - 2, G - 3)
            b_out(G - 1, 1)
            mo, m = G - 2, G - 1
            c_tr(mo, 0, C.g_ready, 4 * mo + 3)
            c_tr(mo, 1, C.hl_ready, 4 * mo + 1)
            pe.wait_ge(X.resid_done, G)
            ln_transposes(C, m)
            c_fc(m, 0, C.hl_ready, 4 * mo + 3)
            c_fc(m, 1, C.g_ready, 4 * m + 1)
            c_out(mo, 0, ps_s[0])
            c_out(mo, 1, ps_s[0])
            c_tr(m, 0, C.g_ready, 4 * m + 3)
            c_out(m, 0, ps_s[1])
            c_tr(m, 1, C.hl_ready, 4 * m + 1)
            c_out(m, 1, ps_s[1])

        @block.scalar
        def _(act):
            def copy(out, in_):
                return nc.scalar.activation(out, in_, ACT.Copy)

            def x_hi(ph, n):
                act.wait_ge(ph.lnt_done, n + 1)
                wait_if(act, ph.pj_ready, n * ph.U)
                copy(ph.norm.xh[:, :, :], ps_x[:, :].rearrange("p (c n) -> p c n", c=DC)).then_inc(ph.xh_ready, 1)

            def exp(ph, i, t):
                act.wait_ge(ph.subbed, i * ph.T + t + 1)
                nc.scalar.activation(prob[:, t % 4, :], prob[:, t % 4, :], ACT.Exp, scale=SCALE).then_inc(ph.exped, 1)

            def pt_copy(ph, i, t):
                act.wait_ge(ph.transposed, i * ph.T + t + 1)
                wait_if(act, ph.av_done, i * ph.T + max(t - 1, 0))
                copy(probT[:, t % 2, :], ps_t[:, :]).then_inc(ph.pt_ready, 1)

            def o_hi(ph, i, t):
                b, q = ph.tile(t)
                act.wait_ge(ph.av_done, i * ph.T + t + 1)
                wait_if(act, ph.out_ready, NB * i)
                copy(oh[:, b, 2 * q:2 * q + 2, :],
                     ps_o[t % 2][:, 0:2 * P].rearrange("p (j n) -> p j n", j=2)).then_inc(ph.oh_ready, 1)

            def a_v(n, b):
                act.wait_ge(A.pj_ready, n * A.U + 4 + b + 1)
                if not (isinstance(n, int) and n == 0):
                    act.wait_ge(A.av_done, (n - 1) * T1 + A.tiles_of(b))
                copy(vA[:, b, :], ps_p[b][:, :]).then_inc(A.v_ready, 1)

            def a_place(n, c):
                act.wait_ge(A.rotated, 4 * n + c + 1)
                if not (isinstance(n, int) and n == 0):
                    act.wait_ge(A.s_ready, (n - 1) * T1 + NB * (c // 2 + 1))
                for j in range(2):
                    pair = 2 * (c // 2) + j
                    for ab in range(2):
                        if c % 2 == 1:
                            last = copy(q_t[HD * ab:HD * ab + HD, pair, :], ropec[HD * j:HD * j + HD, c, ab, :])
                            continue
                        for h in range(2):
                            row, src = HD * ab + 32 * h, HD * j + 32 * h
                            last = copy(k_t[row:row + 32, pair, :, h, :],
                                        ropec[src:src + 32, c, ab, :].rearrange("p (b n) -> p b n", b=NB))
                last.then_inc(A.qk_ready, 1)

            def w2_split_hi(p):
                act.wait_ge(ld_w2, 16 * (p + 1))
                copy(w2[:, 0, bass.ds(p, 1), :].rearrange("p a n -> p (a n)"), stage[:, :]).then_inc(w2_hi, 1)

            def w1_split_hi(ld, k):
                act.wait_ge(ld, 16)
                cols = slice(k * I1, (k + 1) * I1)
                copy(w1h[:, :, cols], w1raw[:, :, cols]).then_inc(w1h_ready, 1)

            w1_split_hi(ld_w1a, 0)
            x_hi(A, 0)
            w1_split_hi(ld_w1b, 1)
            w1_split_hi(ld_w1c, 2)
            act.wait_ge(ld_wo, 16)
            copy(woh[:, :, :], woraw[:, :, :]).then_inc(woh_done, 1)
            act.wait_ge(k_zeroed, 1)
            for c in range(4):
                a_place(0, c)
            a_v(0, 0)

            def a_step(i):
                n = i + 1
                exp(A, i, 0)
                exp(A, i, 1)
                if isinstance(i, int) and i == 0:
                    act.wait_ge(w1l_ready, 3)
                    act.wait_ge(wo_ready, 1)
                w2_split_hi(i)
                a_v(i, 1)
                pt_copy(A, i, 0)
                x_hi(A, n)
                exp(A, i, 2)
                o_hi(A, i, 0)
                pt_copy(A, i, 1)
                exp(A, i, 3)
                o_hi(A, i, 1)
                pt_copy(A, i, 2)
                a_place(n, 0)
                o_hi(A, i, 2)
                pt_copy(A, i, 3)
                a_place(n, 1)
                o_hi(A, i, 3)
                a_place(n, 2)
                a_v(n, 0)
                a_place(n, 3)
            a_step(0)
            with act.Fori(1, G - 1) as i:
                a_step(i)

            def ctx_hi(n):
                act.wait_ge(ld_ctx, 16 * (n + 1))
                wait_if(act, X.pj_ready, n * X.U)
                copy(ch[:, :, :], craw[:, :, :]).then_inc(X.ch_done, 1)

            def b_v(n, b, s):
                u = 10 * b + s
                act.wait_ge(X.pj_ready, n * X.U + u + 1)
                if isinstance(n, int) and n == 0:
                    if b == 1:
                        act.wait_ge(A.av_done, T1 * G)
                else:
                    act.wait_ge(X.av_done, (n - 1) * T2 + X.tiles_of(b))
                copy(vB[:, b, s * 512:(s + 1) * 512], ps_p[u % 2][:, :]).then_inc(X.v_ready, 1)

            def b_q(n, c):
                act.wait_ge(X.pj_ready, n * X.U + 2 + c + 1)
                wait_if(act, X.s_ready, n * T2)
                copy(q_t[:, 2 * c:2 * c + 2, :], ps_p[c % 2][:, :].rearrange("p (j n) -> p j n", j=2)
                     ).then_inc(X.q_ready, 1)

            def b_k(n, c):
                act.wait_ge(X.pj_ready, n * X.U + 6 + c + 1)
                wait_if(act, X.s_ready, n * T2)
                for h in range(2):
                    r = slice(HD * h, HD * h + HD)
                    last = copy(k_t[r, 2 * c:2 * c + 2, :, h, :],
                                ps_p[c % 2][r, :].rearrange("p (j b n) -> p j b n", j=2, b=NB))
                last.then_inc(X.ka_ready, 1)

            i = G - 1
            exp(A, i, 0)
            exp(A, i, 1)
            a_v(i, 1)
            ctx_hi(0)
            exp(A, i, 2)
            pt_copy(A, i, 0)
            act.wait_ge(A.pj_ready, A.U * G)
            x_hi(X, 0)
            o_hi(A, i, 0)
            pt_copy(A, i, 1)
            exp(A, i, 3)
            b_v(0, 0, 0)
            o_hi(A, i, 1)
            b_v(0, 0, 1)
            pt_copy(A, i, 2)
            act.wait_ge(A.s_ready, T1 * G)
            b_q(0, 0)
            b_q(0, 1)
            o_hi(A, i, 2)
            pt_copy(A, i, 3)
            b_q(0, 2)
            b_q(0, 3)
            o_hi(A, i, 3)
            b_k(0, 0)
            b_k(0, 1)
            w2_split_hi(WP - 1)

            def abs_sum(k):
                act.wait_ge(ld_f, 32)
                wait_if(act, abs_summed, k)
                nc.scalar.activation(stage[:, :], fraw[:, k // 2, k % 2 * F:(k % 2 + 1) * F], ACT.Abs,
                                     accum_out=asum[:, k:k + 1]).then_inc(abs_summed, 1)

            def c_gelu(m, b):
                for s in range(2):
                    act.wait_ge(C.pj_ready, m * C.U + 2 * b + s + 1)
                    if not (isinstance(m, int) and m == 0):
                        act.wait_ge(C.gt_ready, 2 * (NB * (m - 1) + b + 1))
                    nc.scalar.activation(g[b][:, s * 512:(s + 1) * 512], ps_p[s][:, :], ACT.Gelu
                                         ).then_inc(C.g_ready, 1)

            def c_hi(m, b):
                if not (isinstance(m, int) and m == 0):
                    act.wait_ge(C.out_ready, NB * (m - 1) + b + 1)
                for s in range(2):
                    act.wait_ge(C.gt_ready, 2 * (NB * m + b) + s + 1)
                    copy(hTh[:, b, 4 * s:4 * s + 4, :], ps_p[s][:, :].rearrange("p (j n) -> p j n", j=4)
                         ).then_inc(C.hh_ready, 1)

            def b_step(i, n, m, mo):
                exp(X, i, 0)
                exp(X, i, 1)
                exp(X, i, 2)
                b_v(i, 1, 0)
                b_v(i, 1, 1)
                if n is not None:
                    x_hi(X, n)
                pt_copy(X, i, 0)
                exp(X, i, 3)
                if n is not None:
                    ctx_hi(n)
                if mo is not None:
                    c_hi(mo, 0)
                o_hi(X, i, 0)
                if m is None:
                    abs_sum(0)
                exp(X, i, 4)
                pt_copy(X, i, 1)
                if m is not None:
                    x_hi(C, m)
                exp(X, i, 5)
                o_hi(X, i, 1)
                pt_copy(X, i, 2)
                if m is None:
                    abs_sum(1)
                if mo is not None:
                    c_hi(mo, 1)
                exp(X, i, 6)
                o_hi(X, i, 2)
                pt_copy(X, i, 3)
                if m is None:
                    abs_sum(2)
                exp(X, i, 7)
                o_hi(X, i, 3)
                pt_copy(X, i, 4)
                if m is None:
                    abs_sum(3)
                o_hi(X, i, 4)
                if m is None:
                    b_v(n, 0, 0)
                else:
                    c_gelu(m, 0)
                pt_copy(X, i, 5)
                if m is None:
                    b_v(n, 0, 1)
                else:
                    c_gelu(m, 1)
                pt_copy(X, i, 6)
                o_hi(X, i, 5)
                if n is not None:
                    if m is not None:
                        b_v(n, 0, 0)
                        b_v(n, 0, 1)
                    b_q(n, 0)
                    b_q(n, 1)
                o_hi(X, i, 6)
                pt_copy(X, i, 7)
                if n is not None:
                    b_q(n, 2)
                    b_q(n, 3)
                o_hi(X, i, 7)
                if n is not None:
                    b_k(n, 0)
                    b_k(n, 1)
            b_step(0, 1, None, None)
            b_step(1, 2, 0, None)
            act.wait_ge(cb_summed, 1)
            copy(cb[:, :], ps_p[0][:, 0:D]).then_inc(cb_ready, 1)
            b_step(2, 3, 1, 0)
            with act.Fori(3, G - 1) as i:
                b_step(i, i + 1, i - 1, i - 2)
            b_step(G - 1, None, G - 2, G - 3)
            mo, m = G - 2, G - 1
            c_hi(mo, 0)
            c_hi(mo, 1)
            x_hi(C, m)
            c_gelu(m, 0)
            c_gelu(m, 1)
            c_hi(m, 0)
            c_hi(m, 1)

        @block.vector
        def _(dve):
            tt = nc.vector.tensor_tensor

            def x_row(b):
                return x_sb[:, b, :] if isinstance(b, int) else x_sb[:, bass.ds(b, 1), :].rearrange("p a d -> p (a d)")

            def x_stats(ph, n):
                for b in range(NB):
                    last = nc.vector.bn_stats(ph.norm.stats[:, b, :], x_row(n * NB + b))
                last.then_inc(ph.stats_done, 1)
                dve.wait_ge(ph.stats_done, n + 1)
                nc.vector.memset(scratch[:, :], 0.0)
                for b in range(NB):
                    last = nc.vector.bn_aggr(ph.norm.mv[:, b, :], ph.norm.stats[:, b, :])
                last.then_inc(ph.aggr_done, 1)
                dve.wait_ge(ph.aggr_done, n + 1)
                nc.vector.tensor_scalar(ph.norm.vareps[:, :], ph.norm.mv[:, :, 1], LN_EPS, None, ALU.add
                                        ).then_inc(ph.vareps_done, 1)

            def x_norm(ph, n):
                dve.wait_ge(ph.rstd_ready, n + 1)
                wait_if(dve, ph.lnt_done, n)
                for b in range(NB):
                    last = nc.vector.tensor_scalar(ph.norm.xn[:, b, :], x_row(n * NB + b), ph.norm.mv[:, b, 0:1],
                                                   ph.norm.rstd[:, b:b + 1], ALU.subtract, ALU.mult)
                last.then_inc(ph.xn_ready, 1)

            def x_lo(ph, n):
                dve.wait_ge(ph.xh_ready, n + 1)
                tt(ph.norm.xl[:, :, :], ps_x[:, :].rearrange("p (c n) -> p c n", c=DC), f32(ph.norm.xh[:, :, :]),
                   ALU.subtract).then_inc(ph.xl_ready, 1)

            def max_sub(ph, i, t):
                dve.wait_ge(ph.s_ready, i * ph.T + t + 1)
                s = ps_s[t % 2][:, :].rearrange("p (h k) -> p h k", h=TH)
                nc.vector.reduce_max(mx[:, t % 4, :], s, AX_X).then_inc(ph.maxed, 1)
                dve.wait_ge(ph.maxed, i * ph.T + t + 1)
                if t >= 4:
                    dve.wait_ge(ph.transposed, i * ph.T + t - 3)
                elif not (isinstance(i, int) and i == 0):
                    dve.wait_ge(ph.transposed, (i - 1) * ph.T + ph.T - 3 + t)
                tt(prob[:, t % 4, :].rearrange("p (h k) -> p h k", h=TH), s, bcast(mx[:, t % 4, :], P), ALU.subtract
                   ).then_inc(ph.subbed, 1)

            def row_sum(ph, i, t):
                dve.wait_ge(ph.exped, i * ph.T + t + 1)
                nc.vector.reduce_sum(sm[:, t % 4, :], prob[:, t % 4, :].rearrange("p (h k) -> p h k", h=TH), AX_X
                                     ).then_inc(ph.summed, 1)
                dve.wait_ge(ph.summed, i * ph.T + t + 1)
                nc.vector.reciprocal(rc[:, t % 4, :], sm[:, t % 4, :]).then_inc(ph.rc_ready, 1)

            def o_lo(ph, i, t):
                b, q = ph.tile(t)
                dve.wait_ge(ph.oh_ready, i * ph.T + t + 1)
                tt(ol[:, b, 2 * q:2 * q + 2, :],
                   ps_o[t % 2][:, 0:2 * P].rearrange("p (j n) -> p j n", j=2),
                   f32(oh[:, b, 2 * q:2 * q + 2, :]), ALU.subtract).then_inc(ph.ol_ready, 1)

            def resid(ph, i, bank):
                dve.wait_ge(ph.out_ready, NB * i + NB)
                xs = x_sb[:, bass.ds(NB * i, NB), :]
                tt(xs, bank[:, :].rearrange("p (b d) -> p b d", b=NB), xs, ALU.add).then_inc(ph.resid_done, 1)

            def a_rope(n, c):
                dve.wait_ge(A.pj_ready, n * A.U + c + 1)
                if not (isinstance(n, int) and n == 0):
                    dve.wait_ge(A.qk_ready, 4 * (n - 1) + c + 1)
                wait_if(dve, A.rotated, 4 * n + max(c - 1, 0))
                bank = ps_p[c % 2][:, :].rearrange("p (a n) -> p a n", n=P)
                for dst, slot, tab in ((ropec, c, cos_t), (ropes, c % 2, sin_t)):
                    last = tt(dst[:, slot, :, :].rearrange("p a (b n) -> p (a b) n", n=P), bank,
                              tab.unsqueeze(1).to_broadcast([P, 4, P]), ALU.mult)
                last.then_inc(A.roped, 1)

            dve.wait_ge(ld_x0, 16)
            x_stats(A, 0)
            x_norm(A, 0)

            def w1_split_lo(k):
                dve.wait_ge(w1h_ready, k + 1)
                cols = slice(k * I1, (k + 1) * I1)
                tt(w1l[:, :, cols], w1raw[:, :, cols], f32(w1h[:, :, cols]), ALU.subtract).then_inc(w1l_ready, 1)

            w1_split_lo(0)
            x_lo(A, 0)
            w1_split_lo(1)
            dve.wait_ge(ld_c, 16)
            nc.vector.tensor_copy(ident_b[:, :], ident).then_inc(masks_ready, 1)
            dve.wait_ge(ld_m, 16)
            for k, m in enumerate((mask_w, mask_c)):
                nc.vector.tensor_copy(m[:, :, :], mask_raw[:, k, :].unsqueeze(1).to_broadcast([P, TH, P])
                                      ).then_inc(masks_ready, 1)
            a_rope(0, 0)
            w1_split_lo(2)
            for c in range(1, 4):
                a_rope(0, c)
            dve.wait_ge(ld_xr, 16)
            x_stats(A, 1)
            x_norm(A, 1)

            def a_step(i, ph, m):
                n = i + 1
                max_sub(A, i, 0)
                max_sub(A, i, 1)
                row_sum(A, i, 0)
                if not (isinstance(i, int) and i == 0):
                    resid(A, i - 1, ps_x)
                row_sum(A, i, 1)
                max_sub(A, i, 2)
                x_lo(A, n)
                max_sub(A, i, 3)
                row_sum(A, i, 2)
                a_rope(n, 0)
                row_sum(A, i, 3)
                o_lo(A, i, 0)
                a_rope(n, 1)
                o_lo(A, i, 1)
                a_rope(n, 2)
                x_stats(ph, m)
                o_lo(A, i, 2)
                a_rope(n, 3)
                if ph is X:
                    dve.wait_ge(A.lnt_done, G)
                x_norm(ph, m)
                o_lo(A, i, 3)
            a_step(0, A, 2)
            with dve.Fori(1, G - 2) as i:
                a_step(i, A, i + 2)
            a_step(G - 2, X, 0)

            def b_k(n, c):
                dve.wait_ge(X.pj_ready, n * X.U + 6 + c + 1)
                wait_if(dve, X.s_ready, n * T2)
                for h in range(2):
                    r = slice(HD * h, HD * h + HD)
                    last = nc.vector.tensor_copy(k_t[r, 2 * c:2 * c + 2, :, h, :],
                                                 ps_p[c % 2][r, :].rearrange("p (j b n) -> p j b n", j=2, b=NB))
                last.then_inc(X.kd_ready, 1)

            i = G - 1
            max_sub(A, i, 0)
            max_sub(A, i, 1)
            row_sum(A, i, 0)
            resid(A, i - 1, ps_x)
            max_sub(A, i, 2)
            row_sum(A, i, 1)
            max_sub(A, i, 3)
            x_lo(X, 0)
            row_sum(A, i, 2)
            x_stats(X, 1)
            row_sum(A, i, 3)
            o_lo(A, i, 0)
            x_norm(X, 1)
            for t in range(1, T1):
                o_lo(A, i, t)
            dve.wait_ge(A.s_ready, T1 * G)
            b_k(0, 2)
            b_k(0, 3)
            resid(A, i, ps_x)

            def thresholds():
                dve.wait_ge(gam_summed, 1)
                nc.vector.reduce_sum(gam[:, :], ps_x[:, 0:4].rearrange("p (m k) -> p m k", m=2), AX_X
                                     ).then_inc(thr_step, 1)
                dve.wait_ge(thr_step, 1)
                nc.vector.tensor_scalar(thr[:, :], gam[:, :], 1.0 / (D * F), GAMMA_EPS, ALU.mult, ALU.add
                                        ).then_inc(thr_step, 1)
                dve.wait_ge(thr_step, 2)
                nc.vector.tensor_scalar(nthr[:, :], thr[:, :], -0.5, None, ALU.mult).then_inc(thr_step, 1)
                dve.wait_ge(thr_step, 3)
                nc.vector.tensor_scalar(thr[:, :], nthr[:, :], -1.0, None, ALU.mult).then_inc(thr_step, 1)
                dve.wait_ge(thr_step, 4)
            def ternarise(k):
                m = k // 2
                raw = fraw[:, m, k % 2 * F:(k % 2 + 1) * F]
                dst = wfc[:, k, :] if m == 0 else wpj[:, 4 * (k - 2):4 * (k - 1), :].rearrange("p j n -> p (j n)")
                wait_if(dve, tern_ready, k)
                nc.vector.tensor_scalar(g[1][:, :], raw, nthr[:, m:m + 1], None, ALU.is_lt).then_inc(tern_neg, 1)
                dve.wait_ge(tern_neg, k + 1)
                nc.vector.scalar_tensor_tensor(out=dst, in0=raw, scalar=thr[:, m:m + 1], in1=g[1][:, :],
                                               op0=ALU.is_gt, op1=ALU.subtract).then_inc(tern_ready, 1)

            def bias_parts():
                dve.wait_ge(ld_ln, 32)
                dve.wait_ge(tern_ready, 2)
                nc.vector.tensor_copy(bh[:, :, :], bcast(lnb_col[:, :], P)).then_inc(bh_ready, 1)
                dve.wait_ge(bh_ready, 1)
                tt(bl[:, :, :], bcast(lnb_col[:, :], P), f32(bh[:, :, :]), ALU.subtract).then_inc(bl_ready, 1)

            def g_stats(m, b):
                dve.wait_ge(C.g_ready, 2 * (NB * m + b + 1))
                for s in range(2):
                    last = nc.vector.bn_stats(gstats[:, b, s, :], g[b][:, s * 512:(s + 1) * 512])
                last.then_inc(C.gstats_done, 1)
                dve.wait_ge(C.gstats_done, NB * m + b + 1)
                nc.vector.memset(scratch[:, :], 0.0)
                nc.vector.bn_aggr(gmv[:, b, :], gstats[:, b, :, :].rearrange("p s k -> p (s k)")).then_inc(C.gaggr_done, 1)
                dve.wait_ge(C.gaggr_done, NB * m + b + 1)
                nc.vector.tensor_scalar(gvareps[:, b:b + 1], gmv[:, b, 1:2], LN_EPS, None, ALU.add
                                        ).then_inc(C.gvareps_done, 1)

            def g_norm(m, b):
                dve.wait_ge(C.grstd_ready, NB * m + b + 1)
                nc.vector.tensor_scalar(g[b][:, :], g[b][:, :], gmv[:, b, 0:1], grstd[:, b:b + 1],
                                        ALU.subtract, ALU.mult).then_inc(C.gscaled, 1)

            def h_lo(m, b):
                for s in range(2):
                    dve.wait_ge(C.hh_ready, 2 * (NB * m + b) + s + 1)
                    tt(hTl[:, b, 4 * s:4 * s + 4, :], ps_p[s][:, :].rearrange("p (j n) -> p j n", j=4),
                       f32(hTh[:, b, 4 * s:4 * s + 4, :]), ALU.subtract).then_inc(C.hl_ready, 1)

            def ffn_resid(m, bank):
                dve.wait_ge(C.cb_added, m + 1)
                resid(C, m, bank)

            def b_step(i, ahead, n2, m, mo):
                first = m is None
                max_sub(X, i, 0)
                max_sub(X, i, 1)
                row_sum(X, i, 0)
                if m is not None:
                    resid(X, i - 1, ps_x)
                max_sub(X, i, 2)
                row_sum(X, i, 1)
                if m is not None:
                    dve.wait_ge(X.resid_done, m + 1)
                    nc.vector.memset(scratch[:, :], 0.0)
                    x_stats(C, m)
                max_sub(X, i, 3)
                if m is not None:
                    x_norm(C, m)
                row_sum(X, i, 2)
                if ahead:
                    x_lo(X, i + 1)
                max_sub(X, i, 4)
                row_sum(X, i, 3)
                max_sub(X, i, 5)
                if mo is not None:
                    h_lo(mo, 0)
                row_sum(X, i, 4)
                o_lo(X, i, 0)
                if m is not None:
                    x_lo(C, m)
                max_sub(X, i, 6)
                o_lo(X, i, 1)
                row_sum(X, i, 5)
                if mo is not None:
                    h_lo(mo, 1)
                max_sub(X, i, 7)
                o_lo(X, i, 2)
                row_sum(X, i, 6)
                row_sum(X, i, 7)
                o_lo(X, i, 3)
                if mo is not None:
                    ffn_resid(mo, ps_x)
                if m is not None:
                    g_stats(m, 0)
                if n2 is not None:
                    x_stats(X, n2)
                o_lo(X, i, 4)
                if first:
                    thresholds()
                    ternarise(0)
                if m is not None:
                    g_norm(m, 0)
                    g_stats(m, 1)
                o_lo(X, i, 5)
                if first:
                    ternarise(1)
                if n2 is not None:
                    x_norm(X, n2)
                if m is not None:
                    g_norm(m, 1)
                if first:
                    ternarise(2)
                o_lo(X, i, 6)
                if first:
                    ternarise(3)
                o_lo(X, i, 7)
                if ahead:
                    b_k(i + 1, 2)
                    b_k(i + 1, 3)
                if first:
                    bias_parts()
            dve.wait_ge(A.resid_done, G)
            b_step(0, True, 2, None, None)
            b_step(1, True, 3, 0, None)
            b_step(2, True, 4, 1, 0)
            with dve.Fori(3, G - 2) as i:
                b_step(i, True, i + 2, i - 1, i - 2)
            b_step(G - 2, True, None, G - 3, G - 4)
            b_step(G - 1, False, None, G - 2, G - 3)
            mo, m = G - 2, G - 1
            resid(X, m, ps_x)
            dve.wait_ge(X.resid_done, G)
            x_stats(C, m)
            h_lo(mo, 0)
            x_norm(C, m)
            h_lo(mo, 1)
            x_lo(C, m)
            for b in range(NB):
                g_stats(m, b)
                if b:
                    h_lo(m, 0)
                g_norm(m, b)
                dve.wait_ge(C.gscaled, NB * m + b + 1)
                tt(g[b][:, :], g[b][:, :], lnw_bc[:, :], ALU.mult).then_inc(C.gn_ready, 1)
            ffn_resid(mo, ps_s[0])
            h_lo(m, 1)
            ffn_resid(m, ps_s[1])

        @block.gpsimd
        def _(pool):
            tt = nc.gpsimd.tensor_tensor

            def x_rstd(ph, n):
                pool.wait_ge(ph.vareps_done, n + 1)
                tt(ph.norm.rstd[:, :], ph.norm.vareps[:, :], neghalf[:, :], ALU.pow).then_inc(ph.rstd_ready, 1)

            def p_norm(ph, i, t):
                pool.wait_ge(ph.rc_ready, i * ph.T + t + 1)
                p = prob[:, t % 4, :].rearrange("p (h k) -> p h k", h=TH)
                tt(p, p, bcast(rc[:, t % 4, :], P), ALU.mult).then_inc(ph.normed, 1)

            def a_rotate(n, c):
                pool.wait_ge(A.roped, 4 * n + c + 1)
                mc, ms = ropec[:, c, :, :], ropes[:, c % 2, :, :]
                for ab, op in ((0, ALU.subtract), (1, ALU.add)):
                    last = tt(mc[:, ab, :], mc[:, ab, :], ms[:, 1 - ab, :], op)
                last.then_inc(A.rotated, 1)

            def w2_split_lo(p):
                pool.wait_ge(w2_hi, p + 1)
                hi, lo = (w2[:, k, bass.ds(p, 1), :].rearrange("p a n -> p (a n)") for k in range(2))
                tt(lo, stage[:, :], f32(hi), ALU.subtract).then_inc(w2_ready, 1)

            nc.gpsimd.memset(neghalf[:, :], -0.5)
            nc.gpsimd.memset(ones_t[:, :], 1.0).then_inc(ones_ready, 1)
            pool.wait_ge(ones_ready, 1)
            x_rstd(A, 0)
            nc.gpsimd.memset(k_t[:, :, :, :, :], 0.0).then_inc(k_zeroed, 1)
            for c in range(4):
                a_rotate(0, c)
            x_rstd(A, 1)
            pool.wait_ge(woh_done, 1)
            tt(wol[:, :, :], woraw[:, :, :], f32(woh[:, :, :]), ALU.subtract).then_inc(wo_ready, 1)

            def a_step(i, ph, m):
                n = i + 1
                p_norm(A, i, 0)
                p_norm(A, i, 1)
                w2_split_lo(i)
                p_norm(A, i, 2)
                a_rotate(n, 0)
                p_norm(A, i, 3)
                a_rotate(n, 1)
                a_rotate(n, 2)
                x_rstd(ph, m)
                a_rotate(n, 3)
            a_step(0, A, 2)
            with pool.Fori(1, G - 2) as i:
                a_step(i, A, i + 2)
            a_step(G - 2, X, 0)

            def ctx_lo(n):
                pool.wait_ge(X.ch_done, n + 1)
                tt(cl[:, :, :], craw[:, :, :], f32(ch[:, :, :]), ALU.subtract).then_inc(X.cl_ready, 1)

            p_norm(A, G - 1, 0)
            ctx_lo(0)
            p_norm(A, G - 1, 1)
            p_norm(A, G - 1, 2)
            x_rstd(X, 1)
            p_norm(A, G - 1, 3)
            pool.wait_ge(A.s_ready, T1 * G)
            pool.wait_ge(A.normed, T1 * G)
            nc.gpsimd.memset(k_t[64:96, :, :, 0, :], 0.0).then_inc(k_zeroed, 1)
            pool.wait_ge(k_zeroed, 2)
            nc.gpsimd.memset(k_t[32:64, :, :, 1, :], 0.0).then_inc(k_zeroed, 1)
            pool.wait_ge(k_zeroed, 3)
            w2_split_lo(WP - 1)

            def g_rstd(m, b):
                pool.wait_ge(C.gvareps_done, NB * m + b + 1)
                tt(grstd[:, b:b + 1], gvareps[:, b:b + 1], neghalf[:, 0:1], ALU.pow).then_inc(C.grstd_ready, 1)

            def g_weight(m, b):
                pool.wait_ge(C.gscaled, NB * m + b + 1)
                tt(g[b][:, :], g[b][:, :], lnw_bc[:, :], ALU.mult).then_inc(C.gn_ready, 1)

            def add_bias_row(m):
                pool.wait_ge(C.xn_ready, m + 1)
                xs = x_sb[:, bass.ds(NB * m, NB), :]
                tt(xs, xs, cb[:, :].unsqueeze(1).to_broadcast([P, NB, D]), ALU.add).then_inc(C.cb_added, 1)

            def b_step(i, ahead, n2, m, mo):
                p_norm(X, i, 0)
                p_norm(X, i, 1)
                if m is not None:
                    x_rstd(C, m)
                p_norm(X, i, 2)
                p_norm(X, i, 3)
                if ahead:
                    ctx_lo(i + 1)
                p_norm(X, i, 4)
                if mo is not None:
                    add_bias_row(mo)
                for t in range(5, T2):
                    p_norm(X, i, t)
                if m is not None:
                    g_rstd(m, 0)
                if n2 is not None:
                    x_rstd(X, n2)
                if m is not None:
                    g_weight(m, 0)
                    g_rstd(m, 1)
                    g_weight(m, 1)
            b_step(0, True, 2, None, None)
            pool.wait_ge(ld_ln, 32)
            b_step(1, True, 3, 0, None)
            pool.wait_ge(cb_ready, 1)
            b_step(2, True, 4, 1, 0)
            with pool.Fori(3, G - 2) as i:
                b_step(i, True, i + 2, i - 1, i - 2)
            b_step(G - 2, True, None, G - 3, G - 4)
            b_step(G - 1, False, None, G - 2, G - 3)
            mo, m = G - 2, G - 1
            x_rstd(C, m)
            add_bias_row(mo)
            add_bias_row(m)
            for b in range(NB):
                g_rstd(m, b)


def _constants():
    import numpy as np
    inv = (1.0 / np.float32(10000.0) ** (np.arange(0, HD, 2, dtype=np.float32) / np.float32(HD))).astype(np.float32)
    ang = (np.arange(T, dtype=np.float32)[None, :] * inv[:, None]).astype(np.float32)
    cos, sin = np.tile(np.cos(ang), (TH, 1)), np.tile(np.sin(ang), (TH, 1))
    q, k = np.arange(T)[:, None], np.arange(T)[None, :]
    window = np.where((k <= q) & (k > q - 64), 0.0, -1e30)
    causal = np.where(k <= q, 0.0, -1e30)
    return np.concatenate([cos, sin, np.eye(P), window, causal], axis=1).astype(np.float32)


def kernel(x, ctx_1024, L0_attn_Wqkv, L0_attn_Wout, L0_xattn_w_q, L0_xattn_w_k, L0_xattn_w_v, L0_xattn_w_o,
           L0_ffn_W_fc, L0_ffn_ln_w, L0_ffn_ln_b, L0_ffn_W_proj):
    import numpy as np
    import concourse.bacc as bacc
    from concourse.bass_utils import run_bass_kernel_spmd

    wqkv = np.asarray(L0_attn_Wqkv)
    qk = wqkv[:, :2 * I1].reshape(D, 2, 2, TH, 2, 32)[:, ::-1].transpose(0, 2, 1, 4, 3, 5).reshape(D, 2 * I1)
    wqkv = np.concatenate([qk, wqkv[:, 2 * I1:]], axis=1)
    proj = [np.asarray(w).T.reshape(DC, P, I2) for w in (L0_xattn_w_q, L0_xattn_w_k, L0_xattn_w_v)]
    wo = np.asarray(L0_xattn_w_o).T.reshape(2, 4, P, D).transpose(0, 2, 1, 3).reshape(2, P, 4 * D)
    arrays = {
        "x": np.asarray(x).reshape(B * T, D),
        "ctxT": np.asarray(ctx_1024).reshape(B * T, D).T,
        "wqkv": wqkv,
        "wout": np.asarray(L0_attn_Wout),
        "wx": np.concatenate(proj + [wo], axis=0),
        "wfcT": np.asarray(L0_ffn_W_fc).T,
        "wprojT": np.asarray(L0_ffn_W_proj).T,
        "lnw": np.asarray(L0_ffn_ln_w),
        "lnb": np.ascontiguousarray(np.asarray(L0_ffn_ln_b).reshape(FC, P).T),
        "tables": _constants(),
    }
    arrays = {k: np.ascontiguousarray(v) for k, v in arrays.items()}
    nc = bacc.Bacc("TRN2", target_bir_lowering=False, num_devices=1)
    aps = [nc.dram_tensor(k, v.shape, mybir.dt.from_np(v.dtype), kind="ExternalInput").ap() for k, v in arrays.items()]
    out = nc.dram_tensor("out", (B * T, D), F32, kind="ExternalOutput").ap()
    decoder_program(nc, *aps, out)
    r = run_bass_kernel_spmd(nc, [arrays], core_ids=[0])
    return r.results[0]["out"].reshape(B, T, D)
```
